# Optimizing a Trainium2 kernel written in Bass

```python
import numpy as np
import jax
import jax.numpy as jnp

def _softmax(x, axis=-1):
    return jax.nn.softmax(x, axis=axis)

def _gelu(x):
    return jax.nn.gelu(x, approximate=True)

def _silu(x):
    return jax.nn.silu(x)

def _sigmoid(x):
    return jax.nn.sigmoid(x)

def _layernorm(x, axis=-1, eps=1e-05):
    m = jnp.mean(x, axis=axis, keepdims=True)
    v = jnp.var(x, axis=axis, keepdims=True)
    return (x - m) / jnp.sqrt(v + eps)

def _scatter_add(tgt, idx, src, axis=0):
    return tgt.at[idx].add(src)

def _segment_sum(src, seg, n):
    return jax.ops.segment_sum(src, seg, n)
kernel_name = 'mk_conv_preact_d4_conv_nhwc256_r4_ca880c'

def setup_inputs(seed: int=0):
    np.random.seed(seed)
    _w = jnp.asarray

    def _rec_inputs():
        import jax
        import jax.numpy as jnp
        _gk = jax.random.key(seed)
        x = -8.268e-05 + 0.9999 * jax.random.normal(jax.random.fold_in(_gk, 1), (8, 28, 28, 64), jnp.float32)
        return x
    x = _rec_inputs()

    def _L0_conv_setup():
        import jax, jax.numpy as jnp
        import numpy as np
        WS = 7
        SH = 3
        NH = 8

        def _shift_attn_mask(H, W):
            img = np.zeros((H, W), dtype=np.float32)
            slices = [(0, -WS), (-WS, -SH), (-SH, None)]
            cnt = 0
            for hs in slices:
                for ws in slices:
                    img[hs[0]:hs[1], ws[0]:ws[1]] = cnt
                    cnt += 1
            nH, nW = (H // WS, W // WS)
            m = img.reshape(nH, WS, nW, WS).transpose(0, 2, 1, 3).reshape(nH * nW, WS * WS)
            diff = m[:, None, :] - m[:, :, None]
            return np.where(diff != 0, np.float32(-100.0), np.float32(0.0))
        key = jax.random.key(seed)
        ks = jax.random.split(key, 6)
        B, H, W, C = (16, 28, 28, 64)
        N = WS * WS
        return {'input': jax.random.normal(ks[0], (B, H, W, C), jnp.float32), 'qkv_weight': jax.random.normal(ks[1], (3 * C, C), jnp.float32) * 0.02, 'qkv_bias': jax.random.normal(ks[2], (3 * C,), jnp.float32) * 0.02, 'proj_weight': jax.random.normal(ks[3], (C, C), jnp.float32) * 0.02, 'proj_bias': jax.random.normal(ks[4], (C,), jnp.float32) * 0.02, 'relative_position_bias': jax.random.normal(ks[5], (1, NH, N, N), jnp.float32) * 0.02}
    _L0_conv_all = _L0_conv_setup()
    _L0_conv_in = {k: v for k, v in _L0_conv_all.items() if k in ('qkv_weight', 'qkv_bias', 'proj_weight', 'proj_bias', 'relative_position_bias')}
    del _L0_conv_all

    def _L1_conv_setup():
        import jax, jax.numpy as jnp
        import numpy as np
        from jax import lax
        KH, KW, PAD = (3, 3, 1)

        def _sign_pm1(v):
            return jnp.where(v > 0, jnp.float32(1.0), jnp.float32(-1.0)).astype(v.dtype)
        key = jax.random.key(seed)
        k1, k2, k3 = jax.random.split(key, 3)
        x = jax.random.normal(k1, (32, 56, 56, 64), dtype=jnp.float32)
        kernel = jax.random.normal(k2, (KH, KW, 64, 64), dtype=jnp.float32) * 0.05
        bias = jax.random.normal(k3, (64,), dtype=jnp.float32) * 0.01
        return {'x': x, 'kernel': kernel, 'bias': bias}
    _L1_conv_all = _L1_conv_setup()
    _L1_conv_in = {k: v for k, v in _L1_conv_all.items() if k in ('kernel', 'bias')}
    del _L1_conv_all

    def _L2_conv_setup():
        import jax, jax.numpy as jnp
        import numpy as np
        key = jax.random.key(seed)
        k1, k2 = jax.random.split(key)
        inputs = jax.random.normal(k1, (32, 56, 56, 64), dtype=jnp.float32)
        kernel = jax.random.normal(k2, (3, 3, 64, 64), dtype=jnp.float32) * 0.05
        return {'inputs': inputs, 'kernel': kernel}
    _L2_conv_all = _L2_conv_setup()
    _L2_conv_in = {k: v for k, v in _L2_conv_all.items() if k in ('kernel',)}
    del _L2_conv_all

    def _L3_conv_setup():
        import jax, jax.numpy as jnp
        import numpy as np
        D_MODEL = 64
        D_CONV = 4
        EXPAND = 2
        D_INNER = EXPAND * D_MODEL

        def silu(v):
            return v * jax.nn.sigmoid(v)
        key = jax.random.key(seed)
        k0, k1, k2, k3, k4 = jax.random.split(key, 5)
        B, H, W = (4, 32, 32)
        x = jax.random.normal(k0, (B, H, W, D_MODEL), jnp.float32)
        W_in = jax.random.normal(k1, (2 * D_INNER, D_MODEL), jnp.float32) * 0.02
        conv_w = jax.random.normal(k2, (D_INNER, 1, D_CONV), jnp.float32) * 0.1
        conv_b = jax.random.normal(k3, (D_INNER,), jnp.float32) * 0.02
        W_out = jax.random.normal(k4, (D_MODEL, D_INNER), jnp.float32) * 0.02
        return {'x': x, 'W_in': W_in, 'conv_w': conv_w, 'conv_b': conv_b, 'W_out': W_out}
    _L3_conv_all = _L3_conv_setup()
    _L3_conv_in = {k: v for k, v in _L3_conv_all.items() if k in ('W_in', 'conv_w', 'conv_b', 'W_out')}
    del _L3_conv_all
    return {'x': x, 'L0_conv_qkv_weight': _L0_conv_in['qkv_weight'], 'L0_conv_qkv_bias': _L0_conv_in['qkv_bias'], 'L0_conv_proj_weight': _L0_conv_in['proj_weight'], 'L0_conv_proj_bias': _L0_conv_in['proj_bias'], 'L0_conv_relative_position_bias': _L0_conv_in['relative_position_bias'], 'L1_conv_kernel': _L1_conv_in['kernel'], 'L1_conv_bias': _L1_conv_in['bias'], 'L2_conv_kernel': _L2_conv_in['kernel'], 'L3_conv_W_in': _L3_conv_in['W_in'], 'L3_conv_conv_w': _L3_conv_in['conv_w'], 'L3_conv_conv_b': _L3_conv_in['conv_b'], 'L3_conv_W_out': _L3_conv_in['W_out']}

def reference(x, L0_conv_qkv_weight, L0_conv_qkv_bias, L0_conv_proj_weight, L0_conv_proj_bias, L0_conv_relative_position_bias, L1_conv_kernel, L1_conv_bias, L2_conv_kernel, L3_conv_W_in, L3_conv_conv_w, L3_conv_conv_b, L3_conv_W_out):
    import jax
    import jax.numpy as jnp

    def _L0_conv_ref(input, qkv_weight, qkv_bias, proj_weight, proj_bias, relative_position_bias):
        import jax, jax.numpy as jnp
        import numpy as np
        WS = 7
        SH = 3
        NH = 8

        def _shift_attn_mask(H, W):
            img = np.zeros((H, W), dtype=np.float32)
            slices = [(0, -WS), (-WS, -SH), (-SH, None)]
            cnt = 0
            for hs in slices:
                for ws in slices:
                    img[hs[0]:hs[1], ws[0]:ws[1]] = cnt
                    cnt += 1
            nH, nW = (H // WS, W // WS)
            m = img.reshape(nH, WS, nW, WS).transpose(0, 2, 1, 3).reshape(nH * nW, WS * WS)
            diff = m[:, None, :] - m[:, :, None]
            return np.where(diff != 0, np.float32(-100.0), np.float32(0.0))
        B, H, W, C = input.shape
        d = C // NH
        nH, nW = (H // WS, W // WS)
        num_windows = nH * nW
        N = WS * WS
        x = jnp.roll(input, (-SH, -SH), axis=(1, 2))
        x = x.reshape(B, nH, WS, nW, WS, C).transpose(0, 1, 3, 2, 4, 5)
        x = x.reshape(B * num_windows, N, C)
        qkv = x @ qkv_weight.T + qkv_bias
        qkv = qkv.reshape(B * num_windows, N, 3, NH, d).transpose(2, 0, 3, 1, 4)
        q, k, v = (qkv[0], qkv[1], qkv[2])
        scale = jnp.asarray(d, x.dtype) ** (-0.5)
        attn = jnp.einsum('whnd,whmd->whnm', q * scale, k) + relative_position_bias
        attn_mask = jnp.asarray(_shift_attn_mask(H, W))
        attn = attn.reshape(B, num_windows, NH, N, N) + attn_mask[None, :, None]
        attn = jax.nn.softmax(attn.reshape(B * num_windows, NH, N, N), axis=-1)
        out = jnp.einsum('whnm,whmd->whnd', attn, v)
        out = out.transpose(0, 2, 1, 3).reshape(B * num_windows, N, C)
        out = out @ proj_weight.T + proj_bias
        out = out.reshape(B, nH, nW, WS, WS, C).transpose(0, 1, 3, 2, 4, 5)
        out = out.reshape(B, H, W, C)
        out = jnp.roll(out, (SH, SH), axis=(1, 2))
        return out

    def _L1_conv_ref(x, kernel, bias):
        import jax, jax.numpy as jnp
        import numpy as np
        from jax import lax
        KH, KW, PAD = (3, 3, 1)

        def _sign_pm1(v):
            return jnp.where(v > 0, jnp.float32(1.0), jnp.float32(-1.0)).astype(v.dtype)
        xp = jnp.pad(x, ((0, 0), (PAD, PAD), (PAD, PAD), (0, 0)))
        bin_k = _sign_pm1(kernel)
        alpha = jnp.mean(jnp.abs(kernel), axis=(0, 1, 2))
        bin_x = _sign_pm1(xp)
        beta = jnp.mean(jnp.abs(xp), axis=3, keepdims=True)
        K = lax.reduce_window(beta, jnp.float32(0.0), lax.add, (1, KH, KW, 1), (1, 1, 1, 1), 'VALID') / (KH * KW)
        Ka = K * alpha
        conv = lax.conv_general_dilated(bin_x, bin_k, window_strides=(1, 1), padding='VALID', dimension_numbers=('NHWC', 'HWIO', 'NHWC'))
        return conv * Ka + bias

    def _L2_conv_ref(inputs, kernel):
        import jax, jax.numpy as jnp
        import numpy as np
        w = jnp.clip(kernel, -1.0, 1.0)
        binary_kernel = w + jax.lax.stop_gradient(jnp.sign(w) - w)
        out = jax.lax.conv_general_dilated(inputs, binary_kernel, window_strides=(1, 1), padding='SAME', rhs_dilation=(1, 1), dimension_numbers=('NHWC', 'HWIO', 'NHWC'))
        return out

    def _L3_conv_ref(x, W_in, conv_w, conv_b, W_out):
        import jax, jax.numpy as jnp
        import numpy as np
        D_MODEL = 64
        D_CONV = 4
        EXPAND = 2
        D_INNER = EXPAND * D_MODEL

        def silu(v):
            return v * jax.nn.sigmoid(v)
        B, H, W, C = x.shape
        L = H * W
        x_flat = x.reshape(B, L, C)
        xz = jnp.einsum('blc,dc->bld', x_flat, W_in)
        x_branch, z_branch = jnp.split(xz, 2, axis=-1)
        u = jax.lax.conv_general_dilated(x_branch.transpose(0, 2, 1), conv_w, window_strides=(1,), padding=[(D_CONV - 1, 0)], dimension_numbers=('NCH', 'OIH', 'NCH'), feature_group_count=D_INNER)
        u = (u + conv_b[None, :, None]).transpose(0, 2, 1)
        u = silu(u)
        y1 = u
        y2 = jnp.flip(jnp.flip(u, axis=1), axis=1)
        u_t = u.reshape(B, H, W, -1).transpose(0, 2, 1, 3).reshape(B, L, -1)
        y3 = u_t.reshape(B, W, H, -1).transpose(0, 2, 1, 3).reshape(B, L, -1)
        y4 = jnp.flip(jnp.flip(u_t, axis=1), axis=1).reshape(B, W, H, -1).transpose(0, 2, 1, 3).reshape(B, L, -1)
        y = (y1 + y2 + y3 + y4) * silu(z_branch)
        out = jnp.einsum('bld,cd->blc', y, W_out)
        return out.reshape(B, H, W, C)

    def _gn(v, G=32, eps=1e-05):
        B_, H_, W_, C_ = v.shape
        g = v.reshape(B_, H_, W_, G, C_ // G)
        m = jnp.mean(g, axis=(1, 2, 4), keepdims=True)
        s = jnp.var(g, axis=(1, 2, 4), keepdims=True)
        return ((g - m) / jnp.sqrt(s + eps)).reshape(v.shape)

    def _ln_c(v, eps=1e-06):
        m = jnp.mean(v, axis=-1, keepdims=True)
        s = jnp.var(v, axis=-1, keepdims=True)
        return (v - m) / jnp.sqrt(s + eps)

    def _ln_t(v, eps=1e-05):
        m = jnp.mean(v, axis=-1, keepdims=True)
        s = jnp.var(v, axis=-1, keepdims=True)
        return (v - m) / jnp.sqrt(s + eps)

    def _to_tokens(v):
        B_, H_, W_, C_ = v.shape
        return v.reshape(B_, H_ * W_, C_)

    def _from_tokens(t, like):
        return t.reshape(like.shape)
    x = x + _L0_conv_ref(_gn(x), L0_conv_qkv_weight, L0_conv_qkv_bias, L0_conv_proj_weight, L0_conv_proj_bias, L0_conv_relative_position_bias)
    x = x + _L1_conv_ref(_gn(x), L1_conv_kernel, L1_conv_bias)
    x = x + _L2_conv_ref(_gn(x), L2_conv_kernel)
    x = x + _L3_conv_ref(_gn(x), L3_conv_W_in, L3_conv_conv_w, L3_conv_conv_b, L3_conv_W_out)
    return x

_drawn_inputs = setup_inputs


def setup_inputs(seed=0):
    import zlib

    import numpy as np

    out = dict(_drawn_inputs(seed))
    spreads = {}
    factors = {'L0_conv_relative_position_bias': 30.627,
     'L1_conv_bias': 8.0,
     'L3_conv_W_in': 8.0,
     'L3_conv_conv_w': 8.0,
     'L3_conv_conv_b': 8.0,
     'L3_conv_W_out': 8.0}
    for name, (base, spread) in spreads.items():
        noise = np.random.default_rng([zlib.crc32(name.encode()), seed]).standard_normal(out[name].shape)
        drawn = base * np.exp(spread * noise) if base else spread * noise
        out[name] = jnp.asarray(drawn.astype(out[name].dtype))
    for name, factor in factors.items():
        out[name] = (out[name] * factor).astype(out[name].dtype)
    return out
```

```python
from contextlib import ExitStack

import numpy as np

import concourse.bass as bass
from concourse import mybir

ALU = mybir.AluOpType
ACT = mybir.ActivationFunctionType
AXX = mybir.AxisListType.X
F32 = mybir.dt.float32
BF16 = mybir.dt.bfloat16

P = 128
C = 64
HW = 28
TOK = HW * HW
NG = 4
WS = 7
SH = 3
NW = HW // WS
WT = WS * WS
RT = NW * WT
NH = 8
HD = C // NH
NWIN = NW * NW
WP = 64 + WT
HALF = TOK // 2
HR = HW // 2
PAD = HW + 2
NTAP = 9
DI = 2 * C
EPS = 1e-5
SCALE = HD ** -0.5

CI = dict(ident=(0, P), avg=(P, P), diff=(2 * P, P), ones=(3 * P, P), fold=(4 * P, WT), kmask=(4 * P + WT, 4))
NCI = 4 * P + WT + 4
WI, at_ = {}, 0
for name_, n_ in (("wq", P), ("wk", P), ("wve", C), ("wvo", C), ("wp", P), ("bq", 1), ("bk", 1), ("bv", 1),
                  ("bp", 1), ("b1", 1), ("cb", 1), ("wx", P), ("wz", P), ("cw", 2 * P), ("wo", C)):
    WI[name_] = (at_, n_)
    at_ += n_
NWI = at_


def program(nc, x_in, cst_in, wts_in, ker1_in, ker2_in, qfix_in, kfix_in, out):
    ctx = ExitStack()
    with ctx:
        def sb(name, shape, dt=F32):
            return ctx.enter_context(nc.sbuf_tensor(name, shape, dt))

        def bank(name):
            return ctx.enter_context(nc.psum_tensor(name, [P, 512], F32))

        def sem(name):
            return ctx.enter_context(nc.semaphore(name))

        x = sb("x", [P, NG + 1, HW, HW])
        cst = sb("cst", [P, NCI])
        wts = sb("wts", [P, NWI])
        ker1 = sb("ker1", [P, NTAP, C])
        ker2 = sb("ker2", [P, NTAP, C])

        def cc(name):
            a, n = CI[name]
            return cst[:, a:a + n]

        def ww(name):
            a, n = WI[name]
            return wts[:, a:a + n]

        xn = sb("xn", [P, 2, NW, WS, WS])
        qbd = sb("qbd", [P, NW, 2, NW, P])
        ks = sb("ks", [P, RT])
        kex = sb("kex", [P, 2, 2, 4, RT])
        d = sb("d", [P, 2, NH, 64])
        mx = sb("mx", [P, 2, NH])
        pt = sb("pt", [P, 2, NH, 64])
        vsb = sb("vsb", [P, 2, NW * 4 * 2, 18])
        rc = sb("rc", [P, 2, NH])
        osb = sb("osb", [P, NW, P])
        att = sb("att", [P, NW, WS, WS])
        bqs = sb("bqs", [P, 1])
        bt = sb("bt", [P, 1])
        NJ = 4 * (NG + 1)

        def col(l, g):
            return l * (NG + 1) + g

        st = sb("st", [P, 2, 2, 6])
        mv = sb("mv", [P, NJ, 2])
        sg = sb("sg", [P, NJ, 3])
        ve = sb("ve", [P, NJ])
        mhalf = sb("mhalf", [P, NG])
        rstd = sb("rstd", [P, NJ])
        nmr = sb("nmr", [P, NJ])
        w1 = sb("w1", [P, NTAP, P], BF16)
        asum = sb("asum", [P, C])
        aw = sb("aw", [P, P])
        sg1 = sb("sg1", [P, 2, PAD, PAD], BF16)
        ab = sb("ab", [P, 2, PAD, PAD])
        h1 = sb("h1", [P, 2, PAD, HW])
        h2 = sb("h2", [P, 2, PAD, HW])
        v1 = sb("v1", [P, 2, HW, HW])
        v2 = sb("v2", [P, 2, HW, HW])
        ka = sb("ka", [P, 2, HALF])
        prod = sb("prod", [P, 2, HALF])
        w2 = sb("w2", [P, NTAP, P], BF16)
        parts = sb("parts", [P, 2, 3, PAD, PAD], BF16)
        xf = sb("xf", [P, 2, HW, HW])
        rem = sb("rem", [P, 2, HW, HW])
        SHF = 3
        g12 = sb("g12", [P, 2, P])
        xs = sb("xs", [P, 2, SHF + TOK])
        su = sb("su", [P, 2, HALF])
        sz = sb("sz", [P, 2, HALF])
        yy = sb("yy", [P, 4, HALF])
        res = sb("res", [P, NG, TOK])

        bk = [bank(f"bank{i}") for i in range(8)]
        ps_s, ps_t, ps_o = bk[0:2], bk[2:4], bk[4:6]
        ps_qk, ps_x = bk[6], bk[7]

        ld_x = [sem(f"ld_x{g}") for g in range(NG)]
        ld_c = sem("ld_c")
        ld_w = sem("ld_w")
        ld_k1, ld_k2 = sem("ld_k1"), sem("ld_k2")
        ld_fix = sem("ld_fix")
        init_dve = sem("init_dve")
        init_pool = sem("init_pool")
        small = sem("small")
        pe_bt = sem("pe_bt")
        pe_alpha = sem("pe_alpha")
        asum_ready = sem("asum_ready")
        w1_ready, w2_ready, aw_ready, g12_ready = sem("w1_ready"), sem("w2_ready"), sem("aw_ready"), sem("g12_ready")
        bqs_ready, bt_ready = sem("bqs_ready"), sem("bt_ready")
        gn_stats, gn_mixed, gn_copied, gn_var, gn_rstd, gn_ready = (
            sem(n) for n in ("gn_stats", "gn_mixed", "gn_copied", "gn_var", "gn_rstd", "gn_ready"))
        bn_done = sem("bn_done")
        xn_ready = sem("xn_ready")
        qk_done, q_ready, ks_ready, kex_ready = sem("qk_done"), sem("q_ready"), sem("ks_ready"), sem("kex_ready")
        v_done, v_ready = sem("v_done"), sem("v_ready")
        s_done, max_done, sub_done, t_done, exp_done, pv_done = (
            sem(n) for n in ("s_done", "max_done", "sub_done", "t_done", "exp_done", "pv_done"))
        rc_done, o_ready, ot_done, att_ready, proj_done, res_done = (
            sem(n) for n in ("rc_done", "o_ready", "ot_done", "att_ready", "proj_done", "res_done"))
        sg_ready, ab_ready, h1_done, h_done, v1_done, box_ready = (
            sem(n) for n in ("sg_ready", "ab_ready", "h1_done", "h_done", "v1_done", "box_ready"))
        conv_done, ka_done, ka_ready, prod_done, x_done = (
            sem(n) for n in ("conv_done", "ka_done", "ka_ready", "prod_done", "x_done"))
        xf_ready, p1_ready, rem_ready, p2_ready, p3_ready = (
            sem(n) for n in ("xf_ready", "p1_ready", "rem_ready", "p2_ready", "p3_ready"))
        xs_ready, u_done, z_done, su_ready, sz_ready, y_ready, out_done, res_ready, stored = (
            sem(n) for n in ("xs_ready", "u_done", "z_done", "su_ready", "sz_ready", "y_ready", "out_done",
                             "res_ready", "stored"))

        def pieces(r):
            rows = [(0, WS, WS * r + SH)] if r < NW - 1 else [(0, WS - SH, HW - (WS - SH)), (WS - SH, WS, 0)]
            cols = [(0, HW - SH, SH), (HW - SH, HW, 0)]
            return [(a, b, s, c, e, t) for a, b, s in rows for c, e, t in cols]

        xflat = x[:].rearrange("p g h w -> p g (h w)")

        block = ctx.enter_context(nc.Block())

        @block.sync
        def _(sp):
            for g in range(NG):
                sp.dma_start(xflat[:, g, :], x_in[:, g, :]).then_inc(ld_x[g], 16)
                if g == 1:
                    sp.dma_start(cst[:], cst_in).then_inc(ld_c, 16)
            sp.dma_start(ker1[:], ker1_in).then_inc(ld_k1, 16)
            sp.dma_start(ker2[:], ker2_in).then_inc(ld_k2, 16)
            for g in range(NG):
                for i in range(2):
                    sp.wait_ge(res_ready, 2 * g + i + 1)
                    sp.dma_start(out[:, g, i * HALF:(i + 1) * HALF],
                                 res[:, g, i * HALF:(i + 1) * HALF]).then_inc(stored, 16)
            sp.wait_ge(stored, 16 * 2 * NG)

        @block.gpsimd
        def _(pool):
            pool.memset(mhalf[:], -0.5).then_inc(init_pool, 1)
            pool.memset(osb[:], 0.0).then_inc(init_pool, 1)
            pool.wait_ge(init_pool, 2)
            pool.memset(qbd[0:64, :, 0], 0.0).then_inc(init_pool, 1)
            pool.wait_ge(init_pool, 3)
            pool.memset(qbd[64:P, :, 1], 0.0).then_inc(init_pool, 1)

            def rsqrt(j, n, count):
                pool.wait_ge(gn_var, count)
                pool.tensor_tensor(rstd[:, j:j + n], ve[:, j:j + n], mhalf[:, 0:n], ALU.pow).then_inc(gn_rstd, 1)

            pool.wait_ge(init_pool, 4)
            rsqrt(0, NG, 1)
            pool.memset(ab[:], 0.0).then_inc(init_pool, 1)

            pool.wait_ge(ld_c, 16)

            def mask_keys(R, par):
                pool.wait_ge(ks_ready, R + 1)
                for j in range(2):
                    q = slice(64 * j, 64 * j + 64)
                    if not (isinstance(R, int) and R == 0 and j == 0):
                        pool.wait_ge(kex_ready, R + R + j)
                    pool.tensor_tensor(
                        kex[q, par, j], ks[q, :].rearrange("p (o t) -> p o t", o=1).broadcast_to([64, 4, RT]),
                        cc("kmask")[q, :].rearrange("p (a o) -> p a o", o=1).broadcast_to([64, 4, RT]), ALU.mult)\
                        .then_inc(kex_ready, 1)

            mask_keys(0, 0)
            mask_keys(1, 1)

            def body(g):
                for r in range(NW):
                    mask_keys(g * NW + r + 2, r % 2)

            with pool.Fori(0, NG) as g:
                body(g)

            pool.wait_ge(kex_ready, 2 * NG * NW + 4)
            rsqrt(col(1, 0), NG, 2)
            for g in range(NG):
                s = g % 2
                pool.wait_ge(h_done, g + 1)
                if g >= 2:
                    pool.wait_ge(ka_done, 2 * (g - 1))
                pool.tensor_tensor(v1[:, s], h2[:, s, 0:HW], h2[:, s, 1:HW + 1], ALU.add).then_inc(v1_done, 1)
                pool.wait_ge(v1_done, g + 1)
                pool.tensor_tensor(v2[:, s], v1[:, s], h2[:, s, 2:PAD], ALU.add).then_inc(box_ready, 1)
            for g in range(NG):
                rsqrt(col(2, g), 1, 3 + g)
            for g in range(NG):
                rsqrt(col(3, g), 1, 3 + NG + g)

        @block.scalar
        def _(act):
            act.dma_start(wts[:], wts_in).then_inc(ld_w, 16)
            for r in range(NW):
                for j in range(2):
                    q = slice(64 * (1 - j), 64 * (1 - j) + 64)
                    act.dma_start(qbd[q, r, j], qfix_in[r]).then_inc(ld_fix, 16)
            for j in range(2):
                q = slice(64 * (1 - j), 64 * (1 - j) + 64)
                for par in range(2):
                    act.dma_start(kex[q, par, j], kfix_in[j]).then_inc(ld_fix, 16)

            def evac_qk(R, r):
                act.wait_ge(qk_done, R + 1)
                for j in range(2):
                    for w in range(2):
                        q = slice(64 * j + 32 * w, 64 * j + 32 * w + 32)
                        last = act.activation(qbd[q, r, j, :, 64 * w:64 * w + WT],
                                              ps_qk[q, 0:RT].rearrange("p (a t) -> p a t", a=NW),
                                              ACT.Identity, bias=bqs[q, 0:1], scale=SCALE)
                last.then_inc(q_ready, 1)
                if not (isinstance(R, int) and R == 0):
                    act.wait_ge(kex_ready, 2 * R)
                act.activation(ks[:], ps_qk[:, RT:2 * RT], ACT.Identity, bias=ww("bk")).then_inc(ks_ready, 1)

            def evac_v(R, par):
                act.wait_ge(v_done, R + 1)
                if not (isinstance(R, int) and R < 2):
                    act.wait_ge(pv_done, R * NW - NW)
                for e in range(2):
                    q = slice(64 * e, 64 * e + WT)
                    last = act.activation(vsb[q, par, :, 9 * e:9 * e + HD],
                                          ps_x[q, 0:NW * C].rearrange("p (n d) -> p n d", d=HD), ACT.Identity)
                last.then_inc(v_ready, 1)

            def expo(W, s):
                act.wait_ge(t_done, W + 1)
                if not (isinstance(W, int) and W < 2):
                    act.wait_ge(pv_done, W - 1)
                act.activation(pt[0:WP, s, :, 0:WT],
                               ps_t[s][0:WP, :].rearrange("p (n t) -> p n t", t=64)[:, :, 0:WT],
                               ACT.Exp).then_inc(exp_done, 1)

            def evac_att(R):
                act.wait_ge(ot_done, R + 1)
                if not (isinstance(R, int) and R == 0):
                    act.wait_ge(proj_done, R)
                act.activation(att[:].rearrange("p a b c -> p (a b c)"), ps_x[:, 0:RT], ACT.Identity)\
                   .then_inc(att_ready, 1)

            act.wait_ge(ld_w, 16)
            act.wait_ge(bqs_ready, 1)
            act.wait_ge(init_pool, 4)
            evac_qk(0, 0)
            act.wait_ge(init_dve, 1)
            evac_v(0, 0)
            evac_qk(1, 1)

            def body(g, first):
                for r in range(NW):
                    R = g * NW + r
                    W = g * NWIN + r * NW
                    expo(W, 0)
                    evac_v(R + 1, (r + 1) % 2)
                    expo(W + 1, 1)
                    if not (first and r == 0):
                        evac_att(R - 1)
                    evac_qk(R + 2, (r + 2) % NW)
                    expo(W + 2, 0)
                    expo(W + 3, 1)

            body(0, True)
            with act.Fori(1, NG) as g:
                body(g, False)
            evac_att(NG * NW - 1)

            act.wait_ge(init_pool, 5)

            def absolutes(g):
                act.wait_ge(gn_ready, 2)
                if g >= 2:
                    act.wait_ge(h_done, g - 1)
                act.activation(ab[:, g % 2, 1:1 + HW, 1:1 + HW], x[:, g], ACT.Abs, bias=nmr[:, col(1, g):col(1, g) + 1],
                               scale=rstd[:, col(1, g):col(1, g) + 1]).then_inc(ab_ready, 1)

            def evac_ka(g):
                for i in range(2):
                    u = 2 * g + i
                    act.wait_ge(ka_done, u + 1)
                    if u >= 2:
                        act.wait_ge(prod_done, u - 1)
                    act.activation(ka[:, i], bk[4 + i][:, 0:HALF], ACT.Identity).then_inc(ka_ready, 1)

            def split(g):
                s, j = g % 2, col(2, g)
                act.wait_ge(gn_ready, 3 + g)
                if g >= 2:
                    act.wait_ge(conv_done, 2 * NG + 2 * (g - 1))
                    act.wait_ge(rem_ready, g - 1)
                act.activation(xf[:, s], x[:, g], ACT.Identity, bias=nmr[:, j:j + 1],
                               scale=rstd[:, j:j + 1]).then_inc(xf_ready, 1)
                act.wait_ge(xf_ready, g + 1)
                act.activation(parts[:, s, 0, 1:1 + HW, 1:1 + HW], xf[:, s], ACT.Identity).then_inc(p1_ready, 1)
                act.wait_ge(rem_ready, g + 1)
                act.activation(parts[:, s, 1, 1:1 + HW, 1:1 + HW], rem[:, s], ACT.Identity).then_inc(p2_ready, 1)

            def stack(g):
                j = col(3, g)
                act.wait_ge(gn_ready, 3 + NG + g)
                if g >= 1:
                    act.wait_ge(u_done, 4 * g)
                    act.wait_ge(z_done, 4 * g)
                for w in range(2):
                    q = slice(64 * w, 64 * w + 64)
                    for e in range(2):
                        last = act.activation(xs[64 * e:64 * e + 64, w, SHF + e:SHF + TOK] if e
                                              else xs[0:64, w, SHF:SHF + TOK],
                                              xflat[q, g, 0:TOK - e], ACT.Identity, bias=nmr[q, j:j + 1],
                                              scale=rstd[q, j:j + 1])
                last.then_inc(xs_ready, 1)

            def gates(g):
                for i in range(2):
                    for w in range(2):
                        u = 4 * g + 2 * i + w
                        s = u % 2
                        if u >= 2:
                            act.wait_ge(y_ready, u - 1)
                        act.wait_ge(u_done, u + 1)
                        act.activation(su[:, s], bk[s][:, 0:HALF], ACT.Silu, bias=ww("cb")).then_inc(su_ready, 1)
                        act.wait_ge(z_done, u + 1)
                        act.activation(sz[:, s], bk[2 + s][:, 0:HALF], ACT.Silu).then_inc(sz_ready, 1)

            absolutes(0)
            absolutes(1)
            for g in range(NG):
                evac_ka(g)
                if g + 2 < NG:
                    absolutes(g + 2)
                if g >= 2:
                    split(g - 2)
            split(2)
            split(3)
            for g in range(NG):
                stack(g)
                gates(g)

        @block.tensor
        def _(pe):
            ident = cc("ident")

            def mix(j, n, count, ps):
                pe.wait_ge(gn_stats, count)
                if count > 1:
                    pe.wait_ge(gn_copied, count - 1)
                pe.matmul(ps[:, 0:2 * n], cc("avg"), mv[:, j:j + n, :].rearrange("p n t -> p (n t)"),
                          start=True, stop=True)
                pe.matmul(ps[:, 2 * n:3 * n], cc("diff"), mv[:, j:j + n, 0], start=True, stop=True)\
                  .then_inc(gn_mixed, 1)

            pe.wait_ge(ld_c, 16)
            pe.wait_ge(ld_w, 16)
            mix(0, NG, 1, bk[0])
            pe.matmul(bk[1][:, 0:1], ww("wp"), ww("bv"), start=True, stop=True).then_inc(pe_bt, 1)

            def proj_qk(R, par):
                pe.wait_ge(xn_ready, R + 1)
                if not (isinstance(R, int) and R == 0):
                    pe.wait_ge(q_ready, R)
                    pe.wait_ge(ks_ready, R)
                rhs = xn[:, par].rearrange("p a i j -> p (a i j)")
                for n, name in enumerate(("wq", "wk")):
                    mm = pe.matmul(ps_qk[:, n * RT:(n + 1) * RT], ww(name), rhs, start=True, stop=True)
                mm.then_inc(qk_done, 1)

            def proj_v(R, par):
                pe.wait_ge(xn_ready, R + 1)
                if not (isinstance(R, int) and R < 3):
                    pe.wait_ge(res_done, R - 2)
                elif R > 0:
                    pe.wait_ge(v_ready, R)
                for a in range(NW):
                    lhs = xn[:, par, a].rearrange("p i j -> p (i j)")
                    for e, name in enumerate(("wve", "wvo")):
                        mm = pe.matmul(ps_x[64 * e:64 * e + WT, a * C:(a + 1) * C], lhs, ww(name),
                                       start=True, stop=True)
                mm.then_inc(v_done, 1)

            def scores(W, R, r, par, a):
                s = a % 2
                if a == 0:
                    pe.wait_ge(q_ready, R + 1)
                    pe.wait_ge(kex_ready, 2 * R + 2)
                if not (isinstance(W, int) and W < 2):
                    pe.wait_ge(sub_done, W - 1)
                for j in range(2):
                    mm = pe.matmul(ps_s[s][0:WP, j * 4 * WT:(j + 1) * 4 * WT], qbd[:, r, j, a, 0:WP],
                                   kex[:, par, j, :, a * WT:(a + 1) * WT], start=True, stop=True)
                mm.then_inc(s_done, 1)

            def turn(W, s):
                pe.wait_ge(sub_done, W + 1)
                if not (isinstance(W, int) and W < 2):
                    pe.wait_ge(exp_done, W - 1)
                for hp in range(NH // 2):
                    mm = pe.transpose(ps_t[s][0:WP, hp * P:hp * P + WP],
                                      d[0:WP, s, 2 * hp:2 * hp + 2, :].rearrange("p a b -> p (a b)")[:, 0:WP],
                                      ident[0:WP, 0:WP])
                mm.then_inc(t_done, 1)

            def values(W, R, par, a):
                s = a % 2
                pe.wait_ge(exp_done, W + 1)
                if a == 0:
                    pe.wait_ge(v_ready, R + 1)
                if a % 2 == 0 and not (isinstance(W, int) and W < 4):
                    pe.wait_ge(o_ready, 2 * R + a // 2 - 1)
                o = ps_o[a // 2][0:WP, (a % 2) * 144:(a % 2) * 144 + 144].rearrange("p (w n) -> p w n", w=2)
                for hp in range(NH // 2):
                    lhs = pt[0:WP, s, 2 * hp:2 * hp + 2, :].rearrange("p a b -> p (a b)")[:, 0:WP]
                    n = (a * 4 + hp) * 2
                    mm = pe.matmul(o[:, :, hp * 18:(hp + 1) * 18], lhs, vsb[0:WP, par, n:n + 2, :],
                                   start=True, stop=True)
                mm.then_inc(pv_done, 1)

            def gather(R):
                pe.wait_ge(o_ready, 2 * R + 2)
                pe.wait_ge(v_ready, R + 3 if not (isinstance(R, int) and R == NG * NW - 1) else R + 2)
                for a in range(NW):
                    mm = pe.matmul(ps_x[:, a * WT:(a + 1) * WT], osb[0:WP, a, :], cc("fold")[0:WP, :],
                                   start=True, stop=True)
                mm.then_inc(ot_done, 1)

            def project(R):
                pe.wait_ge(att_ready, R + 1)
                pe.matmul(ps_x[:, 0:RT], ww("wp"), att[:].rearrange("p a i j -> p i a j"),
                          start=True, stop=True).then_inc(proj_done, 1)

            proj_qk(0, 0)
            proj_v(0, 0)
            proj_qk(1, 1)
            pe.wait_ge(ld_fix, 16 * 12)
            pe.wait_ge(init_pool, 4)
            pe.wait_ge(init_dve, 2)
            scores(0, 0, 0, 0, 0)
            scores(1, 0, 0, 0, 1)

            def body(g, first):
                for r in range(NW):
                    R = g * NW + r
                    W = g * NWIN + r * NW
                    par, nxt = r % 2, (r + 1) % 2
                    turn(W, 0)
                    scores(W + 2, R, r, par, 2)
                    if not (first and r == 0):
                        values(W - 1, R - 1, nxt, 3)
                    proj_v(R + 1, nxt)
                    turn(W + 1, 1)
                    scores(W + 3, R, r, par, 3)
                    values(W, R, par, 0)
                    if not (first and r == 0):
                        gather(R - 1)
                    proj_qk(R + 2, par)
                    turn(W + 2, 0)
                    scores(W + 4, R + 1, (r + 1) % NW, nxt, 0)
                    values(W + 1, R, par, 1)
                    if not (first and r == 0):
                        project(R - 1)
                    turn(W + 3, 1)
                    scores(W + 5, R + 1, (r + 1) % NW, nxt, 1)
                    values(W + 2, R, par, 2)

            body(0, True)
            with pe.Fori(1, NG) as g:
                body(g, False)
            last = NG * NW - 1
            values(NG * NWIN - 1, last, 1, 3)
            gather(last)
            project(last)

            pe.wait_ge(gn_stats, 2)
            mix(col(1, 0), NG, 2, bk[7])
            pe.wait_ge(asum_ready, 1)
            pe.matmul(bk[6][:, 0:C], cc("ones"), asum[:], start=True, stop=True).then_inc(pe_alpha, 1)

            def conv(g, i, wt, src, off):
                u = off + 2 * g + i
                if u >= 4:
                    pe.wait_ge(x_done, u - 3)
                n = 0
                for part in range(len(src)):
                    for tap in range(NTAP):
                        ky, kx = tap // 3, tap % 3
                        mm = pe.matmul(bk[u % 4][:, 0:HALF], wt[:, tap, :],
                                       src[part][:, ky + i * HR:ky + (i + 1) * HR, kx:kx + HW],
                                       start=(n == 0), stop=(n == NTAP * len(src) - 1))
                        n += 1
                mm.then_inc(conv_done, 1)

            pe.wait_ge(w1_ready, 1)
            for g in range(NG):
                pe.wait_ge(sg_ready, g + 1)
                conv(g, 0, w1, [sg1[:, g % 2]], 0)
                conv(g, 1, w1, [sg1[:, g % 2]], 0)
                if g == 0:
                    pe.wait_ge(aw_ready, 1)
                pe.wait_ge(box_ready, g + 1)
                for i in range(2):
                    u = 2 * g + i
                    if u >= 2:
                        pe.wait_ge(ka_ready, u - 1)
                    pe.matmul(bk[4 + i][:, 0:HALF], aw[:], v2[:, g % 2, i * HR:(i + 1) * HR, :],
                              start=True, stop=True).then_inc(ka_done, 1)
                if g >= 1:
                    mix(col(2, g - 1), 1, 2 + g, bk[7])
            pe.wait_ge(w2_ready, 1)
            for g in range(NG):
                if g == 0:
                    mix(col(2, NG - 1), 1, 2 + NG, bk[7])
                pe.wait_ge(p1_ready, g + 1)
                pe.wait_ge(p2_ready, g + 1)
                pe.wait_ge(p3_ready, g + 1)
                src = [parts[:, g % 2, k] for k in range(3)]
                conv(g, 0, w2, src, 2 * NG)
                conv(g, 1, w2, src, 2 * NG)
                if g >= 1:
                    mix(col(3, g - 1), 1, 2 + NG + g, bk[7])
            mix(col(3, NG - 1), 1, 2 + 2 * NG, bk[7])
            pe.wait_ge(g12_ready, 1)
            pe.wait_ge(x_done, 4 * NG)
            for g in range(NG):
                pe.wait_ge(xs_ready, g + 1)
                for i in range(2):
                    for w in range(2):
                        u = 4 * g + 2 * i + w
                        s = u % 2
                        a = i * HALF
                        if u >= 2:
                            pe.wait_ge(su_ready, u - 1)
                        pe.matmul(bk[s][:, 0:HALF], g12[:, 0, :], xs[:, w, SHF + a:SHF + a + HALF],
                                  start=True, stop=False)
                        pe.matmul(bk[s][:, 0:HALF], g12[:, 1, :], xs[:, w, SHF - 2 + a:SHF - 2 + a + HALF],
                                  start=False, stop=True).then_inc(u_done, 1)
                        if u >= 2:
                            pe.wait_ge(sz_ready, u - 1)
                        pe.matmul(bk[2 + s][:, 0:HALF], ww("wz")[0:64, :], xs[0:64, w, SHF + a:SHF + a + HALF],
                                  start=True, stop=True).then_inc(z_done, 1)
                    v = 2 * g + i
                    pe.wait_ge(y_ready, 2 * v + 2)
                    if v >= 2:
                        pe.wait_ge(res_ready, v - 1)
                    for w in range(2):
                        mm = pe.matmul(bk[4 + v % 2][64 * w:64 * w + 64, 0:HALF], ww("wo"), yy[:, 2 * (v % 2) + w, :],
                                       start=True, stop=True)
                    mm.then_inc(out_done, 1)

        @block.vector
        def _(dve):
            nsmall = [0]

            def chain(ins):
                nsmall[0] += 1
                ins.then_inc(small, 1)
                dve.wait_ge(small, nsmall[0])

            nbn = [0]

            def moments(g, j):
                b = nbn[0] % 2
                for i in range(2):
                    last = dve.bn_stats(st[:, b, i, :], xflat[:, g, i * HALF:(i + 1) * HALF])
                nbn[0] += 1
                last.then_inc(bn_done, 1)
                dve.wait_ge(bn_done, nbn[0])
                return dve.bn_aggr(mv[:, j, :], st[:, b].rearrange("p a b -> p (a b)"))

            def groups(j, n, count, ps):
                dve.wait_ge(gn_mixed, count)
                dve.tensor_copy(sg[:, j:j + n, 0:2], ps[:, 0:2 * n].rearrange("p (n t) -> p n t", t=2))
                dve.tensor_copy(sg[:, j:j + n, 2], ps[:, 2 * n:3 * n]).then_inc(gn_copied, 1)
                dve.wait_ge(gn_copied, count)
                chain(dve.tensor_tensor(ve[:, j:j + n], sg[:, j:j + n, 2], sg[:, j:j + n, 2], ALU.mult))
                dve.scalar_tensor_tensor(out=ve[:, j:j + n], in0=ve[:, j:j + n], scalar=EPS, in1=sg[:, j:j + n, 1],
                                         op0=ALU.add, op1=ALU.add).then_inc(gn_var, 1)
                dve.wait_ge(gn_rstd, count)
                dve.scalar_tensor_tensor(out=nmr[:, j:j + n], in0=sg[:, j:j + n, 0], scalar=-1.0,
                                         in1=rstd[:, j:j + n], op0=ALU.mult, op1=ALU.mult).then_inc(gn_ready, 1)

            dve.memset(x[:, NG], 0.0)
            chain(dve.memset(vsb[:], 0.0))
            dve.memset(vsb[0:WT, :, :, 8:9], 1.0)
            dve.memset(vsb[64:WP, :, :, 17:18], 1.0).then_inc(init_dve, 1)
            dve.memset(pt[:], 0.0)
            dve.memset(d[:], 0.0).then_inc(init_dve, 1)
            for g in range(NG):
                dve.wait_ge(ld_x[g], 16)
                last = moments(g, g)
            last.then_inc(gn_stats, 1)
            dve.wait_ge(ld_w, 16)
            dve.tensor_scalar(bqs[:], ww("bq"), SCALE, None, ALU.mult).then_inc(bqs_ready, 1)
            dve.wait_ge(pe_bt, 1)
            dve.tensor_tensor(bt[:], bk[1][:, 0:1], ww("bp"), ALU.add).then_inc(bt_ready, 1)
            groups(0, NG, 1, bk[0])
            dve.wait_ge(gn_ready, 1)
            dve.wait_ge(bt_ready, 1)

            def normalise(g, R, r):
                if not (isinstance(R, int) and R < 2):
                    dve.wait_ge(v_done, R - 1)
                for a, b, s, c, e, t in pieces(r):
                    whole = (e - c) // WS if c == 0 else 0
                    runs = [(c, whole, WS)] if whole else []
                    runs.append((c + whole * WS, 1, e - c - whole * WS))
                    for c0, n, m in runs:
                        t0 = t + c0 - c
                        last = dve.tensor_scalar(
                            xn[:, r % 2, c0 // WS:c0 // WS + n, a:b, c0 % WS:c0 % WS + m],
                            x[:, g, s:s + b - a, t0:t0 + n * m].rearrange("p i (n j) -> p n i j", n=n),
                            rstd[:, bass.ds(g, 1)], nmr[:, bass.ds(g, 1)], ALU.mult, ALU.add)
                last.then_inc(xn_ready, 1)

            def shift(W, s):
                dve.wait_ge(s_done, W + 1)
                sc = ps_s[s][0:WP, 0:NH * WT].rearrange("p (h k) -> p h k", k=WT)
                dve.tensor_reduce(mx[0:WP, s], sc, AXX, ALU.max).then_inc(max_done, 1)
                dve.wait_ge(max_done, W + 1)
                if not (isinstance(W, int) and W < 2):
                    dve.wait_ge(t_done, W - 1)
                dve.tensor_tensor(d[0:WP, s, :, 0:WT], sc,
                                  mx[0:WP, s].rearrange("p (h o) -> p h o", o=1).broadcast_to([WP, NH, WT]),
                                  ALU.subtract).then_inc(sub_done, 1)

            def weigh(R, b):
                dve.wait_ge(pv_done, NW * R + 2 * b + 2)
                o = ps_o[b][:, 0:288].rearrange("p (a w h e) -> p a w h e", a=2, w=2, e=9)
                for w in range(2):
                    q = slice(64 * w, 64 * w + WT)
                    last = dve.reciprocal(rc[q], o[q, :, w, :, 8])
                last.then_inc(rc_done, 1)
                dve.wait_ge(rc_done, 2 * R + b + 1)
                if b == 0 and not (isinstance(R, int) and R == 0):
                    dve.wait_ge(ot_done, R)
                for w in range(2):
                    q = slice(64 * w, 64 * w + WT)
                    for a in range(2):
                        last = dve.tensor_tensor(
                            osb[q, 2 * b + a, 64 * w:64 * w + 64].rearrange("p (h e) -> p h e", e=HD),
                            o[q, a, w, :, 0:HD],
                            rc[q, a].rearrange("p (h o) -> p h o", o=1).broadcast_to([WT, NH, HD]), ALU.mult)
                last.then_inc(o_ready, 1)

            def residual(g, R, r):
                dve.wait_ge(proj_done, R + 1)
                y = ps_x[:, 0:RT].rearrange("p (i j) -> p i j", j=HW)
                for a, b, s, c, e, t in pieces(r):
                    xx = x[:, g, s:s + b - a, t:t + e - c]
                    last = dve.scalar_tensor_tensor(out=xx, in0=y[:, a:b, c:e], scalar=bt[:, 0:1], in1=xx,
                                                    op0=ALU.add, op1=ALU.add)
                last.then_inc(res_done, 1)

            dve.memset(rstd[:, NG:NG + 1], 0.0)
            chain(dve.memset(nmr[:, NG:NG + 1], 0.0))
            normalise(0, 0, 0)
            normalise(0, 1, 1)
            dve.wait_ge(init_pool, 4)
            shift(0, 0)

            def body(g, first):
                for r in range(NW):
                    R = g * NW + r
                    W = g * NWIN + r * NW
                    shift(W + 1, 1)
                    normalise(g if r < 2 else g + 1, R + 2, (r + 2) % NW)
                    if not (first and r == 0):
                        weigh(R - 1, 1)
                    shift(W + 2, 0)
                    shift(W + 3, 1)
                    weigh(R, 0)
                    shift(W + 4, 0)
                    if not (first and r == 0):
                        residual(g if r else g - 1, R - 1, (r - 1) % NW)

            body(0, True)
            with dve.Fori(1, NG) as g:
                body(g, False)
            weigh(NG * NW - 1, 1)
            residual(NG - 1, NG * NW - 1, NW - 1)
            dve.wait_ge(res_done, NG * NW)

            for g in range(NG):
                last = moments(g, col(1, g))
            last.then_inc(gn_stats, 1)
            dve.wait_ge(ld_k1, 16)
            k1f = ker1[:].rearrange("p t c -> p (t c)")
            chain(dve.scalar_tensor_tensor(out=h1[:, 0].rearrange("p a b -> p (a b)")[:, 0:NTAP * C], in0=k1f,
                                           scalar=-1.0, in1=k1f, op0=ALU.mult, op1=ALU.max))
            dve.tensor_reduce(asum[:], h1[:, 0].rearrange("p a b -> p (a b)")[:, 0:NTAP * C]
                              .rearrange("p (t c) -> p c t", c=C), AXX, ALU.add).then_inc(asum_ready, 1)
            dve.memset(w1[:], 0.0)
            dve.memset(w2[:], 0.0)
            dve.memset(aw[:], 0.0)
            dve.memset(sg1[:], -0.5)
            dve.memset(parts[:], 0.0)
            chain(dve.memset(xs[:], 0.0))
            for w in range(2):
                q = slice(64 * w, 64 * w + 64)
                last = dve.tensor_scalar(w1[q, :, 64 * w:64 * w + 64], ker1[q], 0.0, 0.5, ALU.is_gt, ALU.subtract)
            last.then_inc(w1_ready, 1)
            dve.wait_ge(pe_alpha, 1)
            for w in range(2):
                q = slice(64 * w, 64 * w + 64)
                last = dve.tensor_scalar(aw[q, 64 * w:64 * w + 64], bk[6][q, 0:C],
                                         4.0 / (NTAP * C) / (NTAP * C), None, ALU.mult)
            last.then_inc(aw_ready, 1)
            groups(col(1, 0), NG, 2, bk[7])
            dve.wait_ge(gn_ready, 2)

            def signs(g):
                if g >= 2:
                    dve.wait_ge(conv_done, 2 * (g - 1))
                dve.tensor_scalar(sg1[:, g % 2, 1:1 + HW, 1:1 + HW], x[:, g], sg[:, col(1, g), 0:1], 0.5,
                                  ALU.is_gt, ALU.subtract).then_inc(sg_ready, 1)

            def horizontal(g):
                s = g % 2
                dve.wait_ge(ab_ready, g + 1)
                dve.tensor_tensor(h1[:, s], ab[:, s, :, 0:HW], ab[:, s, :, 1:HW + 1], ALU.add).then_inc(h1_done, 1)
                dve.wait_ge(h1_done, g + 1)
                if g >= 2:
                    dve.wait_ge(box_ready, g - 1)
                dve.tensor_tensor(h2[:, s], h1[:, s], ab[:, s, :, 2:PAD], ALU.add).then_inc(h_done, 1)

            def finish1(g):
                for i in range(2):
                    u = 2 * g + i
                    xx = xflat[:, g, i * HALF:(i + 1) * HALF]
                    dve.wait_ge(conv_done, u + 1)
                    dve.wait_ge(ka_ready, u + 1)
                    dve.tensor_tensor(prod[:, i], bk[u % 4][:, 0:HALF], ka[:, i], ALU.mult).then_inc(prod_done, 1)
                    dve.wait_ge(prod_done, u + 1)
                    dve.scalar_tensor_tensor(out=xx, in0=prod[:, i], scalar=ww("b1"), in1=xx, op0=ALU.add,
                                             op1=ALU.add).then_inc(x_done, 1)
                dve.wait_ge(x_done, 2 * g + 2)
                moments(g, col(2, g)).then_inc(gn_stats, 1)

            def remainders(g):
                s = g % 2
                dve.wait_ge(xf_ready, g + 1)
                dve.wait_ge(p1_ready, g + 1)
                if g >= 2:
                    dve.wait_ge(p2_ready, g - 1)
                dve.tensor_tensor(rem[:, s], xf[:, s], parts[:, s, 0, 1:1 + HW, 1:1 + HW], ALU.subtract)\
                   .then_inc(rem_ready, 1)
                dve.wait_ge(rem_ready, g + 1)
                dve.wait_ge(p2_ready, g + 1)
                dve.tensor_tensor(parts[:, s, 2, 1:1 + HW, 1:1 + HW], rem[:, s], parts[:, s, 1, 1:1 + HW, 1:1 + HW],
                                  ALU.subtract).then_inc(p3_ready, 1)

            def finish2(g):
                for i in range(2):
                    u = 2 * NG + 2 * g + i
                    xx = xflat[:, g, i * HALF:(i + 1) * HALF]
                    dve.wait_ge(conv_done, u + 1)
                    dve.tensor_tensor(xx, bk[u % 4][:, 0:HALF], xx, ALU.add).then_inc(x_done, 1)
                dve.wait_ge(x_done, 2 * NG + 2 * g + 2)
                moments(g, col(3, g)).then_inc(gn_stats, 1)

            signs(0)
            horizontal(0)
            signs(1)
            horizontal(1)
            dve.wait_ge(ld_k2, 16)
            for w in range(2):
                q = slice(64 * w, 64 * w + 64)
                blk = w2[q, :, 64 * w:64 * w + 64]
                chain(dve.tensor_scalar(blk, ker2[q], 0.0, None, ALU.is_lt))
                last = dve.scalar_tensor_tensor(out=blk, in0=ker2[q], scalar=0.0, in1=blk, op0=ALU.is_gt,
                                                op1=ALU.subtract)
            last.then_inc(w2_ready, 1)
            dve.tensor_tensor(g12[:, 0, :], ww("wx"), ww("cw")[:, 0:P], ALU.mult)
            dve.tensor_tensor(g12[:, 1, :], ww("wx"), ww("cw")[:, P:2 * P], ALU.mult).then_inc(g12_ready, 1)
            for g in range(NG):
                finish1(g)
                if g + 2 < NG:
                    signs(g + 2)
                    horizontal(g + 2)
                if g >= 1:
                    groups(col(2, g - 1), 1, 2 + g, bk[7])
                if g >= 2:
                    remainders(g - 2)
            groups(col(2, NG - 1), 1, 2 + NG, bk[7])
            for g in range(NG):
                finish2(g)
                if g + 2 < NG:
                    remainders(g + 2)
                if g >= 1:
                    groups(col(3, g - 1), 1, 2 + NG + g, bk[7])
            groups(col(3, NG - 1), 1, 2 + 2 * NG, bk[7])
            for g in range(NG):
                for i in range(2):
                    v = 2 * g + i
                    for w in range(2):
                        u = 2 * v + w
                        dve.wait_ge(su_ready, u + 1)
                        dve.wait_ge(sz_ready, u + 1)
                        if v >= 2:
                            dve.wait_ge(out_done, v - 1)
                        dve.scalar_tensor_tensor(out=yy[:, 2 * (v % 2) + w, :], in0=su[:, u % 2], scalar=4.0,
                                                 in1=sz[:, u % 2], op0=ALU.mult, op1=ALU.mult).then_inc(y_ready, 1)
                    dve.wait_ge(out_done, v + 1)
                    dve.tensor_tensor(res[:, g, i * HALF:(i + 1) * HALF], bk[4 + v % 2][:, 0:HALF],
                                      xflat[:, g, i * HALF:(i + 1) * HALF], ALU.add).then_inc(res_ready, 1)


def pair(a):
    n = a.shape[1]
    o = np.zeros((P, 2, n), a.dtype)
    o[:C, 0] = a
    o[C:, 1] = a
    return o


def constants():
    c = np.zeros((P, NCI), np.float32)
    i = np.arange(P)
    c[i, CI["ident"][0] + i] = 1
    for o, s in ((0, 0.5), (1, 0.5)):
        c[i, CI["avg"][0] + (i ^ o)] = 0.5
    c[i, CI["diff"][0] + i] = 0.5
    c[i, CI["diff"][0] + (i ^ 1)] = -0.5
    c[:C, CI["ones"][0]:CI["ones"][0] + C] = 1
    c[C:, CI["ones"][0] + C:CI["ones"][0] + P] = 1
    for w in range(2):
        c[64 * w + np.arange(WT), CI["fold"][0] + np.arange(WT)] = 1
    c[i, CI["kmask"][0] + (i % 32) // HD] = 1
    late = (np.arange(WS) >= WS - SH).astype(int)
    row, col = np.repeat(late, WS), np.tile(late, WS)
    regions = [row == 0, row == 1, col == 0, col == 1]
    regions += [(row == a) & (col == b) for a in range(2) for b in range(2)]
    qfix = np.zeros((NW, 64, NW, P), np.float32)
    q = np.arange(WT)
    for r in range(NW):
        for a in range(NW):
            use = {(0, 0): [], (1, 0): [0, 1], (0, 1): [2, 3], (1, 1): [4, 5, 6, 7]}[(r == NW - 1, a == NW - 1)]
            for w in range(2):
                qfix[r, q, a, 64 * w + q] = 1
                for k in use:
                    qfix[r, WT + k, a, 64 * w:64 * w + WT] = regions[k]
    return c, qfix, np.array(regions)


def kernel(x, L0_conv_qkv_weight, L0_conv_qkv_bias, L0_conv_proj_weight, L0_conv_proj_bias,
           L0_conv_relative_position_bias, L1_conv_kernel, L1_conv_bias, L2_conv_kernel, L3_conv_W_in,
           L3_conv_conv_w, L3_conv_conv_b, L3_conv_W_out):
    import concourse.bacc as bacc
    from concourse.bass_utils import run_bass_kernel_spmd

    f = np.float32
    x = np.asarray(x)
    wqkv, bqkv = np.asarray(L0_conv_qkv_weight), np.asarray(L0_conv_qkv_bias)
    wp, bp = np.asarray(L0_conv_proj_weight), np.asarray(L0_conv_proj_bias)
    rel = np.asarray(L0_conv_relative_position_bias)
    k1, b1 = np.asarray(L1_conv_kernel), np.asarray(L1_conv_bias)
    k2 = np.asarray(L2_conv_kernel)
    win, cw, cb, wo = (np.asarray(a) for a in (L3_conv_W_in, L3_conv_conv_w, L3_conv_conv_b, L3_conv_W_out))

    cst, qfix, regions = constants()
    kfix = np.zeros((2, 64, 4, NW, WT), f)
    for j in range(2):
        kfix[j, 0:WT] = rel[0, 4 * j:4 * j + 4].transpose(1, 0, 2)[:, :, None, :]
        for k, reg in enumerate(regions):
            kfix[j, WT + k] = np.where(reg, 0, -100)

    w = np.zeros((P, NWI), f)

    def put(name, a):
        w[:, WI[name][0]:WI[name][0] + WI[name][1]] = a.reshape(P, -1)

    def by_head_half(a):
        return a.reshape(-1, 2, 2, 32).transpose(0, 2, 1, 3).reshape(-1, P)

    both = lambda v: np.concatenate([v, v])
    put("wq", by_head_half(pair(wqkv[0:C].T)))
    put("wk", by_head_half(pair(wqkv[C:2 * C].T)))
    wv = pair(wqkv[2 * C:].T).reshape(P, 2, 4, 2, HD)
    put("wve", wv[:, :, :, 0].transpose(0, 2, 1, 3))
    put("wvo", wv[:, :, :, 1].transpose(0, 2, 1, 3))
    put("wp", pair(wp.T))
    put("bq", by_head_half(both(bqkv[0:C])[None]))
    put("bk", by_head_half(both(bqkv[C:2 * C])[None]))
    put("bv", both(bqkv[2 * C:]))
    put("bp", both(bp))
    put("b1", both(b1))
    put("cb", cb)
    put("wx", both(win[0:DI].T))
    put("wz", both(win[DI:].T))
    cwt = cw[:, 0, :].T
    put("cw", np.concatenate([np.repeat(cwt[None, [3, 1]], C, 0), np.repeat(cwt[None, [2, 0]], C, 0)]))
    put("wo", wo.T)
    taps = lambda k: np.ascontiguousarray(both(k.reshape(NTAP, C, C).transpose(1, 0, 2)))

    arrays = {
        "x_in": np.ascontiguousarray(x.reshape(NG, 2, TOK, C).transpose(1, 3, 0, 2).reshape(P, NG, TOK)),
        "cst_in": cst, "wts_in": w, "ker1_in": taps(k1), "ker2_in": taps(k2), "qfix_in": qfix,
        "kfix_in": kfix.reshape(2, 64, 4, RT),
    }
    nc = bacc.Bacc("TRN2", target_bir_lowering=False, num_devices=1)
    args = [nc.dram_tensor(n, a.shape, mybir.dt.from_np(a.dtype), kind="ExternalInput").ap()
            for n, a in arrays.items()]
    args.append(nc.dram_tensor("out", (P, NG, TOK), F32, kind="ExternalOutput").ap())
    program(nc, *args)
    r = run_bass_kernel_spmd(nc, [arrays], core_ids=[0])
    y = np.asarray(r.results[0]["out"]).reshape(2, C, NG, HW, HW)
    return np.ascontiguousarray(y.transpose(2, 0, 3, 4, 1).reshape(2 * NG, HW, HW, C))
```

```python
from contextlib import ExitStack

import numpy as np

import concourse.bass as bass
from concourse import mybir

ALU = mybir.AluOpType
ACT = mybir.ActivationFunctionType
AXX = mybir.AxisListType.X
F32 = mybir.dt.float32
BF16 = mybir.dt.bfloat16

P = 128
C = 64
HW = 28
TOK = HW * HW
NG = 4
WS = 7
SH = 3
NW = HW // WS
WT = WS * WS
RT = NW * WT
NH = 8
HD = C // NH
NWIN = NW * NW
WP = 64 + WT
HALF = TOK // 2
HR = HW // 2
PAD = HW + 2
NTAP = 9
DI = 2 * C
EPS = 1e-5
SCALE = HD ** -0.5

CI = dict(ident=(0, P), avg=(P, P), diff=(2 * P, P), ones=(3 * P, P), kmask=(4 * P, 4))
NCI = 4 * P + 4
WI, WIDTHS = {}, []
for part_ in ((("wq", P), ("wk", P), ("wv", P), ("wp", P), ("bq", 1), ("bk", 1), ("bv", 1), ("bp", 1)),
              (("b1", 1), ("cb", 1), ("wx", P), ("wz", P), ("cw", 2 * P), ("wo", C))):
    at_ = 0
    for name_, n_ in part_:
        WI[name_] = (len(WIDTHS), at_, n_)
        at_ += n_
    WIDTHS.append(at_)


def program(nc, x_in, cst_in, wts_in, late_in, ker1_in, ker2_in, qfix_in, kfix_in, out):
    ctx = ExitStack()
    with ctx:
        def sb(name, shape, dt=F32):
            return ctx.enter_context(nc.sbuf_tensor(name, shape, dt))

        def bank(name):
            return ctx.enter_context(nc.psum_tensor(name, [P, 512], F32))

        def sem(name):
            return ctx.enter_context(nc.semaphore(name))

        x = sb("x", [P, NG + 1, HW, HW])
        cst = sb("cst", [P, NCI])
        wts = sb("wts", [P, WIDTHS[0]])
        late = sb("late", [P, WIDTHS[1]])
        ker1 = sb("ker1", [P, NTAP, C])
        ker2 = sb("ker2", [P, NTAP, C])

        def cc(name):
            a, n = CI[name]
            return cst[:, a:a + n]

        def ww(name):
            t, a, n = WI[name]
            return (wts, late)[t][:, a:a + n]

        xn = sb("xn", [P, 2, NW, P])
        qbd = sb("qbd", [P, NW, 2, NW, P])
        ks = sb("ks", [P, RT])
        kex = sb("kex", [P, 2, 2, 4, RT])
        d = sb("d", [P, 2, NH, 64])
        mx = sb("mx", [P, 2, NH])
        pt = sb("pt", [P, 2, NH, 64])
        vsb = sb("vsb", [P, 2, NW * 4 * 2, 18])
        rc = sb("rc", [P, 2, NH])
        osb = sb("osb", [P, NW, C])
        att = sb("att", [P, NW, WS, WS])
        bqs = sb("bqs", [P, 1])
        bt = sb("bt", [P, 1])
        NJ = 4 * (NG + 1)

        def col(l, g):
            return l * (NG + 1) + g

        warm = sb("warm", [P, 1])
        st = sb("st", [P, NG, 2, 6])
        mv = sb("mv", [P, NJ, 2])
        sg = sb("sg", [P, NJ, 3])
        ve = sb("ve", [P, NJ])
        mhalf = sb("mhalf", [P, NG])
        rstd = sb("rstd", [P, NJ])
        nmr = sb("nmr", [P, NJ])
        w1 = sb("w1", [P, NTAP, P], BF16)
        asum = sb("asum", [P, C])
        aw = sb("aw", [P, P])
        sg1 = sb("sg1", [P, 2, PAD, PAD], BF16)
        ab = sb("ab", [P, 2, PAD, PAD])
        h1 = sb("h1", [P, 2, PAD, HW])
        h2 = sb("h2", [P, 2, PAD, HW])
        v1 = sb("v1", [P, 2, HW, HW])
        v2 = sb("v2", [P, 2, HW, HW])
        ka = sb("ka", [P, 2, HALF])
        prod = sb("prod", [P, 2, HALF])
        w2 = sb("w2", [P, NTAP, P], BF16)
        parts = sb("parts", [P, 2, 3, PAD, PAD], BF16)
        xf = sb("xf", [P, 2, HW, HW])
        rem = sb("rem", [P, 2, HW, HW])
        SHF = 3
        g12 = sb("g12", [P, 2, P])
        xs = sb("xs", [P, 2, 2, SHF + TOK])
        su = sb("su", [P, 2, HALF])
        sz = sb("sz", [P, 2, HALF])
        yy = sb("yy", [P, 4, HALF])
        res = sb("res", [P, NG, TOK])

        bk = [bank(f"bank{i}") for i in range(8)]
        ps_s, ps_t, ps_o = bk[0:2], bk[2:4], bk[4:6]
        ps_qk, ps_x = bk[6], bk[7]

        ld_x = [sem(f"ld_x{g}") for g in range(NG)]
        ld_c = sem("ld_c")
        ld_w = sem("ld_w")
        ld_late = sem("ld_late")
        warm_set = sem("warm_set")
        xn_half = sem("xn_half")
        ld_k1, ld_k2 = sem("ld_k1"), sem("ld_k2")
        ld_fix0, ld_fix = sem("ld_fix0"), sem("ld_fix")
        init_dve = sem("init_dve")
        init_pool = sem("init_pool")
        small = sem("small")
        pe_bt = sem("pe_bt")
        pe_alpha = sem("pe_alpha")
        asum_ready = sem("asum_ready")
        w1_ready, w2_ready, aw_ready, g12_ready = sem("w1_ready"), sem("w2_ready"), sem("aw_ready"), sem("g12_ready")
        bqs_ready, bt_ready = sem("bqs_ready"), sem("bt_ready")
        gn_stats, gn_mixed, gn_copied, gn_var, gn_rstd, gn_ready = (
            sem(n) for n in ("gn_stats", "gn_mixed", "gn_copied", "gn_var", "gn_rstd", "gn_ready"))
        bn_done, gn_square = sem("bn_done"), sem("gn_square")
        xn_ready = sem("xn_ready")
        qk_done, q_ready, ks_ready, kex_ready = sem("qk_done"), sem("q_ready"), sem("ks_ready"), sem("kex_ready")
        v_done, v_ready = sem("v_done"), sem("v_ready")
        s_done, max_done, sub_done, t_done, exp_done, pv_done = (
            sem(n) for n in ("s_done", "max_done", "sub_done", "t_done", "exp_done", "pv_done"))
        rc_done, o_ready, ot_done, att_ready, proj_done, res_done = (
            sem(n) for n in ("rc_done", "o_ready", "ot_done", "att_ready", "proj_done", "res_done"))
        sg_ready, ab_ready, h1_done, h_done, v1_done, box_ready = (
            sem(n) for n in ("sg_ready", "ab_ready", "h1_done", "h_done", "v1_done", "box_ready"))
        conv_done, ka_done, ka_ready, prod_done, x_done = (
            sem(n) for n in ("conv_done", "ka_done", "ka_ready", "prod_done", "x_done"))
        xf_ready, p1_ready, rem_ready, p2_ready, p3_ready = (
            sem(n) for n in ("xf_ready", "p1_ready", "rem_ready", "p2_ready", "p3_ready"))
        xs_ready, u_done, z_done, su_ready, sz_ready, y_ready, out_done, res_ready, stored = (
            sem(n) for n in ("xs_ready", "u_done", "z_done", "su_ready", "sz_ready", "y_ready", "out_done",
                             "res_ready", "stored"))

        def pieces(r):
            rows = [(0, WS, WS * r + SH)] if r < NW - 1 else [(0, WS - SH, HW - (WS - SH)), (WS - SH, WS, 0)]
            cols = [(0, HW - SH, SH), (HW - SH, HW, 0)]
            return [(a, b, s, c, e, t) for a, b, s in rows for c, e, t in cols]

        xflat = x[:].rearrange("p g h w -> p g (h w)")

        block = ctx.enter_context(nc.Block())

        @block.sync
        def _(sp):
            sp.dma_start(xflat[:, 0, :], x_in[:, 0, :]).then_inc(ld_x[0], 16)
            sp.dma_start(cst[:], cst_in).then_inc(ld_c, 16)
            for g in range(1, NG):
                sp.dma_start(xflat[:, g, :], x_in[:, g, :]).then_inc(ld_x[g], 16)
            sp.dma_start(ker1[:], ker1_in).then_inc(ld_k1, 16)
            sp.dma_start(ker2[:], ker2_in).then_inc(ld_k2, 16)
            sp.dma_start(late[:], late_in).then_inc(ld_late, 16)
            for g in range(NG):
                for i in range(2):
                    sp.wait_ge(res_ready, 2 * g + i + 1)
                    sp.dma_start(out[:, g, i * HALF:(i + 1) * HALF],
                                 res[:, g, i * HALF:(i + 1) * HALF]).then_inc(stored, 16)
            sp.wait_ge(stored, 16 * 2 * NG)

        @block.gpsimd
        def _(pool):
            pool.memset(mhalf[:], -0.5).then_inc(init_pool, 1)
            pool.memset(xn[:], 0.0).then_inc(init_pool, 1)
            pool.wait_ge(init_pool, 2)
            pool.memset(qbd[0:64, :, 0], 0.0).then_inc(init_pool, 1)
            pool.wait_ge(init_pool, 3)
            pool.memset(qbd[64:P, :, 1], 0.0).then_inc(init_pool, 1)

            def rsqrt(j, n, count):
                pool.wait_ge(gn_var, count)
                pool.tensor_tensor(rstd[:, bass.ds(j, n)], ve[:, bass.ds(j, n)], mhalf[:, 0:n], ALU.pow)\
                    .then_inc(gn_rstd, 1)

            pool.wait_ge(init_pool, 4)
            rsqrt(0, 1, 1)
            pool.memset(osb[:], 0.0).then_inc(init_pool, 1)
            pool.wait_ge(ld_c, 16)
            pool.wait_ge(init_pool, 5)
            pool.wait_ge(gn_rstd, 1)

            def mask_keys(R, par):
                pool.wait_ge(ks_ready, R + 1)
                for j in range(2):
                    q = slice(64 * j, 64 * j + 64)
                    if not (isinstance(R, int) and R == 0 and j == 0):
                        pool.wait_ge(kex_ready, R + R + j)
                    pool.tensor_tensor(
                        kex[q, par, j], ks[q, :].rearrange("p (o t) -> p o t", o=1).broadcast_to([64, 4, RT]),
                        cc("kmask")[q, :].rearrange("p (a o) -> p a o", o=1).broadcast_to([64, 4, RT]), ALU.mult)\
                        .then_inc(kex_ready, 1)

            mask_keys(0, 0)
            mask_keys(1, 1)

            def body(g, first):
                for r in range(NW):
                    R = g * NW + r
                    mask_keys(R + 2, r % 2)
                    if first and r == 1:
                        pool.wait_ge(kex_ready, 2 * R + 6)
                        rsqrt(1, NG - 1, 2)
                        pool.memset(ab[:], 0.0)
                        pool.memset(w1[:], 0.0)
                        pool.memset(w2[:], 0.0)
                        pool.memset(aw[:], 0.0).then_inc(init_pool, 1)
                        pool.wait_ge(gn_rstd, 2)
                        pool.wait_ge(init_pool, 6)
                    if first and r == 2:
                        pool.wait_ge(kex_ready, 2 * R + 6)
                        pool.memset(sg1[:], -0.5)
                        pool.memset(parts[:], 0.0)
                        pool.memset(xs[:], 0.0).then_inc(init_pool, 1)
                        pool.wait_ge(init_pool, 7)

            body(0, True)
            with pool.Fori(1, NG) as g:
                body(g, False)
            pool.wait_ge(kex_ready, 2 * NG * NW + 4)

            def sums(g):
                s = g % 2
                pool.wait_ge(ab_ready, g + 1)
                pool.tensor_tensor(h1[:, s], ab[:, s, :, 0:HW], ab[:, s, :, 1:HW + 1], ALU.add).then_inc(h1_done, 1)
                pool.wait_ge(h1_done, g + 1)
                pool.tensor_tensor(h2[:, s], h1[:, s], ab[:, s, :, 2:PAD], ALU.add).then_inc(h_done, 1)
                pool.wait_ge(h_done, g + 1)
                pool.tensor_tensor(v1[:, s], h2[:, s, 0:HW], h2[:, s, 1:HW + 1], ALU.add).then_inc(v1_done, 1)
                pool.wait_ge(v1_done, g + 1)
                if g >= 2:
                    pool.wait_ge(ka_done, 2 * (g - 1))
                pool.tensor_tensor(v2[:, s], v1[:, s], h2[:, s, 2:PAD], ALU.add).then_inc(box_ready, 1)

            rsqrt(col(1, 0), NG - 1, 3)
            sums(0)
            sums(1)
            rsqrt(col(1, NG - 1), 1, 4)
            sums(2)
            rsqrt(col(2, 0), 1, 5)
            sums(3)
            for g in range(1, NG):
                rsqrt(col(2, g), 1, 5 + g)
            for g in range(NG):
                rsqrt(col(3, g), 1, 9 + g)

        @block.scalar
        def _(act):
            act.dma_start(wts[:], wts_in).then_inc(ld_w, 16)
            def fixed_q(r, signal):
                for j in range(2):
                    act.dma_start(qbd[64 * (1 - j):64 * (2 - j), r, j], qfix_in[r]).then_inc(signal, 16)

            def fixed_k(par, signal):
                for j in range(2):
                    act.dma_start(kex[64 * (1 - j):64 * (2 - j), par, j], kfix_in[j]).then_inc(signal, 16)

            fixed_q(0, ld_fix0)
            fixed_k(0, ld_fix0)
            fixed_k(1, ld_fix)
            for r in range(1, NW):
                fixed_q(r, ld_fix)
            act.wait_ge(warm_set, 1)
            act.activation(warm[:], warm[:], ACT.Exp).then_inc(warm_set, 1)

            def evac_qk(R, r):
                act.wait_ge(qk_done, R + 1)
                for j in range(2):
                    for w in range(2):
                        q = slice(64 * j + 32 * w, 64 * j + 32 * w + 32)
                        last = act.activation(qbd[q, r, j, :, 64 * w:64 * w + WT],
                                              ps_qk[q, 0:RT].rearrange("p (a t) -> p a t", a=NW),
                                              ACT.Identity, bias=bqs[q, 0:1], scale=SCALE)
                last.then_inc(q_ready, 1)
                if not (isinstance(R, int) and R == 0):
                    act.wait_ge(kex_ready, 2 * R)
                act.activation(ks[:], ps_qk[:, RT:2 * RT], ACT.Identity, bias=ww("bk")).then_inc(ks_ready, 1)

            def evac_v(R, par):
                act.wait_ge(v_done, R + 1)
                if not (isinstance(R, int) and R < 2):
                    act.wait_ge(pv_done, R * NW - NW)
                for e in range(2):
                    q = slice(64 * e, 64 * e + WT)
                    last = act.activation(vsb[q, par].rearrange("p (a n) d -> p a n d", a=NW)[:, :, :, 9 * e:9 * e + HD],
                                          ps_x[q, :].rearrange("p (a t n d) -> p t a n d", a=NW, t=2, d=HD)[:, e],
                                          ACT.Identity)
                last.then_inc(v_ready, 1)

            def expo(W, s):
                act.wait_ge(t_done, W + 1)
                if not (isinstance(W, int) and W < 2):
                    act.wait_ge(pv_done, W - 1)
                act.activation(pt[0:WP, s, :, 0:WT],
                               ps_t[s][0:WP, :].rearrange("p (n t) -> p n t", t=64)[:, :, 0:WT],
                               ACT.Exp).then_inc(exp_done, 1)

            def evac_att(R):
                act.wait_ge(ot_done, R + 1)
                if not (isinstance(R, int) and R == 0):
                    act.wait_ge(proj_done, R)
                for w in range(2):
                    for e in range(2):
                        last = act.activation(att[64 * w:64 * w + 64, e::2].rearrange("p a i j -> p a (i j)"),
                                              ps_x[64 * e:64 * e + 64, 0:2 * P]
                                              .rearrange("p (a t) -> p a t", a=2)[:, :, 64 * w:64 * w + WT],
                                              ACT.Identity)
                last.then_inc(att_ready, 1)

            act.wait_ge(ld_w, 16)
            act.wait_ge(bqs_ready, 1)
            act.wait_ge(init_pool, 4)
            evac_qk(0, 0)
            act.wait_ge(init_dve, 1)
            evac_v(0, 0)
            evac_qk(1, 1)

            def body(g, first):
                for r in range(NW):
                    R = g * NW + r
                    W = g * NWIN + r * NW
                    expo(W, 0)
                    evac_v(R + 1, (r + 1) % 2)
                    expo(W + 1, 1)
                    if not (first and r == 0):
                        evac_att(R - 1)
                    evac_qk(R + 2, (r + 2) % NW)
                    expo(W + 2, 0)
                    expo(W + 3, 1)

            body(0, True)
            with act.Fori(1, NG) as g:
                body(g, False)

            def absolutes(g):
                act.wait_ge(gn_ready, 3 if g < NG - 1 else 4)
                if g >= 2:
                    act.wait_ge(h_done, g - 1)
                act.activation(ab[:, g % 2, 1:1 + HW, 1:1 + HW], x[:, g], ACT.Abs,
                               bias=nmr[:, col(1, g):col(1, g) + 1],
                               scale=rstd[:, col(1, g):col(1, g) + 1]).then_inc(ab_ready, 1)

            def evac_ka(g):
                for i in range(2):
                    u = 2 * g + i
                    act.wait_ge(ka_done, u + 1)
                    if u >= 2:
                        act.wait_ge(prod_done, u - 1)
                    act.activation(ka[:, i], bk[4 + i][:, 0:HALF], ACT.Identity).then_inc(ka_ready, 1)

            def split_a(g):
                s, j = g % 2, col(2, g)
                act.wait_ge(gn_ready, 5 + g)
                if g >= 2:
                    act.wait_ge(conv_done, 2 * NG + 2 * (g - 1))
                    act.wait_ge(rem_ready, g - 1)
                act.activation(xf[:, s], x[:, g], ACT.Identity, bias=nmr[:, j:j + 1], scale=rstd[:, j:j + 1])
                act.activation(parts[:, s, 0, 1:1 + HW, 1:1 + HW], x[:, g], ACT.Identity, bias=nmr[:, j:j + 1],
                               scale=rstd[:, j:j + 1]).then_inc(p1_ready, 1)

            def split_b(g):
                s = g % 2
                act.wait_ge(rem_ready, g + 1)
                act.activation(parts[:, s, 1, 1:1 + HW, 1:1 + HW], rem[:, s], ACT.Identity).then_inc(p2_ready, 1)

            def stack(g):
                j = col(3, g)
                act.wait_ge(gn_ready, 9 + g)
                if g >= 2:
                    act.wait_ge(z_done, 4 * (g - 1))
                for w in range(2):
                    q = slice(64 * w, 64 * w + 64)
                    for e in range(2):
                        last = act.activation(xs[64 * e:64 * e + 64, g % 2, w, SHF + e:SHF + TOK],
                                              xflat[q, g, 0:TOK - e], ACT.Identity, bias=nmr[q, j:j + 1],
                                              scale=rstd[q, j:j + 1])
                last.then_inc(xs_ready, 1)

            def gates(g):
                for i in range(2):
                    for w in range(2):
                        u = 4 * g + 2 * i + w
                        s = u % 2
                        if u >= 2:
                            act.wait_ge(y_ready, u - 1)
                        act.wait_ge(u_done, u + 1)
                        act.activation(su[:, s], bk[s][:, 0:HALF], ACT.Silu, bias=ww("cb")).then_inc(su_ready, 1)
                        act.wait_ge(z_done, u + 1)
                        act.activation(sz[:, s], bk[2 + s][:, 0:HALF], ACT.Silu).then_inc(sz_ready, 1)

            act.wait_ge(init_pool, 7)
            absolutes(0)
            evac_att(NG * NW - 1)
            absolutes(1)
            evac_ka(0)
            absolutes(2)
            evac_ka(1)
            absolutes(3)
            evac_ka(2)
            split_a(0)
            evac_ka(3)
            split_b(0)
            for g in range(1, NG):
                split_a(g)
                split_b(g)
            act.wait_ge(ld_late, 16)
            stack(0)
            stack(1)
            gates(0)
            stack(2)
            gates(1)
            stack(3)
            gates(2)
            gates(3)

        @block.tensor
        def _(pe):
            ident = cc("ident")

            def mix(j, n, count, ps):
                pe.wait_ge(gn_stats, count)
                if count > 1:
                    pe.wait_ge(gn_copied, count - 1)
                pe.matmul(ps[:, 0:2 * n], cc("avg"), mv[:, j:j + n, :].rearrange("p n t -> p (n t)"),
                          start=True, stop=True)
                pe.matmul(ps[:, 2 * n:3 * n], cc("diff"), mv[:, j:j + n, 0], start=True, stop=True)\
                  .then_inc(gn_mixed, 1)

            pe.wait_ge(ld_c, 16)
            mix(0, 1, 1, bk[2])
            pe.wait_ge(ld_w, 16)
            pe.matmul(bk[3][:, 0:1], ww("wp"), ww("bv"), start=True, stop=True).then_inc(pe_bt, 1)

            def proj_qk(R, par):
                pe.wait_ge(xn_ready, R + 1)
                if not (isinstance(R, int) and R == 0):
                    pe.wait_ge(q_ready, R)
                    pe.wait_ge(ks_ready, R)
                if isinstance(R, int) and R == 3:
                    pe.wait_ge(gn_copied, 2)
                rhs = xn[:, par, :, 0:WT]
                for n, name in enumerate(("wq", "wk")):
                    mm = pe.matmul(ps_qk[:, n * RT:(n + 1) * RT], ww(name), rhs, start=True, stop=True)
                mm.then_inc(qk_done, 1)

            def proj_v(R, par):
                pe.wait_ge(xn_ready, R + 1)
                if not (isinstance(R, int) and R < 3):
                    pe.wait_ge(res_done, R - 2)
                elif R > 0:
                    pe.wait_ge(v_ready, R)
                for a in range(NW):
                    mm = pe.matmul(ps_x[0:WP, a * P:(a + 1) * P], xn[:, par, a, 0:WP], ww("wv"),
                                   start=True, stop=True)
                mm.then_inc(v_done, 1)

            def scores(W, R, r, par, a):
                s = a % 2
                if a == 0:
                    pe.wait_ge(q_ready, R + 1)
                    pe.wait_ge(kex_ready, 2 * R + 2)
                if not (isinstance(W, int) and W < 2):
                    pe.wait_ge(sub_done, W - 1)
                for j in range(2):
                    mm = pe.matmul(ps_s[s][0:WP, j * 4 * WT:(j + 1) * 4 * WT], qbd[:, r, j, a, 0:WP],
                                   kex[:, par, j, :, a * WT:(a + 1) * WT], start=True, stop=True)
                mm.then_inc(s_done, 1)

            def turn(W, s):
                pe.wait_ge(sub_done, W + 1)
                if not (isinstance(W, int) and W < 2):
                    pe.wait_ge(exp_done, W - 1)
                for hp in range(NH // 2):
                    mm = pe.transpose(ps_t[s][0:WP, hp * P:hp * P + WP],
                                      d[0:WP, s, 2 * hp:2 * hp + 2, :].rearrange("p a b -> p (a b)")[:, 0:WP],
                                      ident[0:WP, 0:WP])
                mm.then_inc(t_done, 1)

            def values(W, R, par, a):
                s = a % 2
                pe.wait_ge(exp_done, W + 1)
                if a == 0:
                    pe.wait_ge(v_ready, R + 1)
                if a % 2 == 0 and not (isinstance(W, int) and W < 4):
                    pe.wait_ge(o_ready, 2 * R + a // 2 - 1)
                o = ps_o[a // 2][0:WP, (a % 2) * 144:(a % 2) * 144 + 144].rearrange("p (w n) -> p w n", w=2)
                for hp in range(NH // 2):
                    lhs = pt[0:WP, s, 2 * hp:2 * hp + 2, :].rearrange("p a b -> p (a b)")[:, 0:WP]
                    n = (a * 4 + hp) * 2
                    mm = pe.matmul(o[:, :, hp * 18:(hp + 1) * 18], lhs, vsb[0:WP, par, n:n + 2, :],
                                   start=True, stop=True)
                mm.then_inc(pv_done, 1)

            def gather(R):
                pe.wait_ge(o_ready, 2 * R + 2)
                pe.wait_ge(v_ready, R + 3 if not (isinstance(R, int) and R == NG * NW - 1) else R + 2)
                for b in range(2):
                    mm = pe.transpose(ps_x[:, b * P:b * P + WP],
                                      osb[0:WP, 2 * b:2 * b + 2, :].rearrange("p a c -> p (a c)"), ident[0:WP, 0:WP])
                mm.then_inc(ot_done, 1)

            def project(R):
                pe.wait_ge(att_ready, R + 1)
                pe.matmul(ps_x[:, 0:RT], ww("wp"), att[:].rearrange("p a i j -> p i a j"),
                          start=True, stop=True).then_inc(proj_done, 1)

            proj_qk(0, 0)
            proj_v(0, 0)
            proj_qk(1, 1)
            pe.wait_ge(ld_fix0, 16 * 4)
            pe.wait_ge(init_pool, 5)
            pe.wait_ge(init_dve, 2)
            scores(0, 0, 0, 0, 0)
            scores(1, 0, 0, 0, 1)

            def body(g, first):
                for r in range(NW):
                    R = g * NW + r
                    W = g * NWIN + r * NW
                    par, nxt = r % 2, (r + 1) % 2
                    turn(W, 0)
                    scores(W + 2, R, r, par, 2)
                    if not (first and r == 0):
                        values(W - 1, R - 1, nxt, 3)
                    proj_v(R + 1, nxt)
                    turn(W + 1, 1)
                    scores(W + 3, R, r, par, 3)
                    values(W, R, par, 0)
                    if not (first and r == 0):
                        gather(R - 1)
                    proj_qk(R + 2, par)
                    turn(W + 2, 0)
                    if first and r == 0:
                        pe.wait_ge(ld_fix, 16 * 8)
                    scores(W + 4, R + 1, (r + 1) % NW, nxt, 0)
                    values(W + 1, R, par, 1)
                    if not (first and r == 0):
                        project(R - 1)
                    turn(W + 3, 1)
                    scores(W + 5, R + 1, (r + 1) % NW, nxt, 1)
                    values(W + 2, R, par, 2)
                    if first and r == 0:
                        pe.wait_ge(q_ready, R + 3)
                        pe.wait_ge(ks_ready, R + 3)
                        mix(1, NG - 1, 2, ps_qk)

            body(0, True)
            with pe.Fori(1, NG) as g:
                body(g, False)
            def conv(g, i, wt, src, off, ready):
                u = off + 2 * g + i
                if i == 0:
                    for signal in ready:
                        pe.wait_ge(signal, g + 1)
                if u >= 4:
                    pe.wait_ge(x_done, u - 3)
                n = 0
                for part in range(len(src)):
                    for tap in range(NTAP):
                        ky, kx = tap // 3, tap % 3
                        mm = pe.matmul(bk[u % 4][:, 0:HALF], wt[:, tap, :],
                                       src[part][:, ky + i * HR:ky + (i + 1) * HR, kx:kx + HW],
                                       start=(n == 0), stop=(n == NTAP * len(src) - 1))
                        n += 1
                mm.then_inc(conv_done, 1)

            def conv1(g, i):
                conv(g, i, w1, [sg1[:, g % 2]], 0, [sg_ready])

            def conv2(g):
                src = [parts[:, g % 2, k] for k in range(3)]
                for i in range(2):
                    conv(g, i, w2, src, 2 * NG, [p1_ready, p2_ready, p3_ready])

            def channel_sums(g):
                pe.wait_ge(box_ready, g + 1)
                for i in range(2):
                    u = 2 * g + i
                    if u >= 2:
                        pe.wait_ge(ka_ready, u - 1)
                    pe.matmul(bk[4 + i][:, 0:HALF], aw[:], v2[:, g % 2, i * HR:(i + 1) * HR, :],
                              start=True, stop=True).then_inc(ka_done, 1)

            last = NG * NW - 1
            values(NG * NWIN - 1, last, 1, 3)
            pe.wait_ge(asum_ready, 1)
            pe.wait_ge(q_ready, NG * NW + 2)
            pe.wait_ge(ks_ready, NG * NW + 2)
            pe.matmul(ps_qk[:, C:2 * C], cc("ones"), asum[:], start=True, stop=True).then_inc(pe_alpha, 1)
            mix(col(1, 0), NG - 1, 3, ps_qk)
            pe.wait_ge(sub_done, NG * NWIN + 1)
            pe.wait_ge(w1_ready, 1)
            conv1(0, 0)
            gather(last)
            conv1(0, 1)
            project(last)
            conv1(1, 0)
            conv1(1, 1)
            pe.wait_ge(aw_ready, 1)
            pe.wait_ge(o_ready, 2 * NG * NW)
            channel_sums(0)
            mix(col(1, NG - 1), 1, 4, bk[7])
            channel_sums(1)
            conv1(2, 0)
            conv1(2, 1)
            mix(col(2, 0), 1, 5, bk[7])
            channel_sums(2)
            conv1(3, 0)
            conv1(3, 1)
            mix(col(2, 1), 1, 6, bk[7])
            channel_sums(3)
            pe.wait_ge(w2_ready, 1)
            mix(col(2, 2), 1, 7, bk[7])
            conv2(0)
            mix(col(2, 3), 1, 8, bk[7])
            conv2(1)
            mix(col(3, 0), 1, 9, bk[7])
            conv2(2)
            mix(col(3, 1), 1, 10, bk[7])
            conv2(3)
            mix(col(3, 2), 1, 11, bk[7])
            pe.wait_ge(g12_ready, 1)
            pe.wait_ge(ld_late, 16)

            def expand(v, w):
                g, u, s, a = v // 2, 2 * v + w, w, (v % 2) * HALF
                if w == 0 and v % 2 == 0:
                    pe.wait_ge(xs_ready, g + 1)
                if u >= 2:
                    pe.wait_ge(su_ready, u - 1)
                else:
                    pe.wait_ge(x_done, 4 * NG - 2)
                t = xs[:, g % 2, w]
                pe.matmul(bk[s][:, 0:HALF], g12[:, 0, :], t[:, SHF + a:SHF + a + HALF], start=True, stop=False)
                pe.matmul(bk[s][:, 0:HALF], g12[:, 1, :], t[:, SHF - 2 + a:SHF - 2 + a + HALF],
                          start=False, stop=True).then_inc(u_done, 1)
                if u >= 2:
                    pe.wait_ge(sz_ready, u - 1)
                else:
                    pe.wait_ge(x_done, 4 * NG)
                pe.matmul(bk[2 + s][:, 0:HALF], ww("wz")[0:64, :], t[0:64, SHF + a:SHF + a + HALF],
                          start=True, stop=True).then_inc(z_done, 1)

            def contract(v):
                pe.wait_ge(y_ready, 2 * v + 2)
                if v >= 2:
                    pe.wait_ge(res_ready, v - 1)
                for w in range(2):
                    mm = pe.matmul(bk[4 + v % 2][64 * w:64 * w + 64, 0:HALF], ww("wo"), yy[:, 2 * (v % 2) + w, :],
                                   start=True, stop=True)
                mm.then_inc(out_done, 1)

            for v in range(2 * NG):
                expand(v, 0)
                if v >= 1:
                    contract(v - 1)
                expand(v, 1)
                if v == 1:
                    mix(col(3, 3), 1, 12, bk[7])
            contract(2 * NG - 1)

        @block.vector
        def _(dve):
            nsmall = [0]

            def chain(ins):
                nsmall[0] += 1
                ins.then_inc(small, 1)
                dve.wait_ge(small, nsmall[0])

            def half_moments(g):
                for i in range(2):
                    last = dve.bn_stats(st[:, bass.ds(g, 1), i, :].rearrange("p o t -> p (o t)"),
                                        xflat[:, g, i * HALF:(i + 1) * HALF])
                last.then_inc(bn_done, 1)

            def merge(g, j, count):
                dve.wait_ge(bn_done, count)
                return dve.bn_aggr(mv[:, j, :], st[:, g].rearrange("p a b -> p (a b)"))

            def moments(g, layer):
                half_moments(g)
                return merge(g, col(layer, g), NG * layer + g + 1)

            def variances(j, n, count, ps):
                jj = bass.ds(j, n)
                dve.wait_ge(gn_mixed, count)
                dve.tensor_copy(sg[:, jj, 0:2], ps[:, 0:2 * n].rearrange("p (n t) -> p n t", t=2))
                dve.tensor_copy(sg[:, jj, 2], ps[:, 2 * n:3 * n]).then_inc(gn_copied, 1)
                dve.wait_ge(gn_copied, count)
                dve.tensor_tensor(ve[:, jj], sg[:, jj, 2], sg[:, jj, 2], ALU.mult).then_inc(gn_square, 1)
                dve.wait_ge(gn_square, count)
                dve.scalar_tensor_tensor(out=ve[:, jj], in0=ve[:, jj], scalar=EPS, in1=sg[:, jj, 1],
                                         op0=ALU.add, op1=ALU.add).then_inc(gn_var, 1)

            def shifts(j, n, count):
                jj = bass.ds(j, n)
                dve.wait_ge(gn_rstd, count)
                dve.scalar_tensor_tensor(out=nmr[:, jj], in0=sg[:, jj, 0], scalar=-1.0, in1=rstd[:, jj],
                                         op0=ALU.mult, op1=ALU.mult).then_inc(gn_ready, 1)

            dve.memset(warm[:], 0.0).then_inc(warm_set, 1)
            dve.memset(x[:, NG], 0.0)
            dve.memset(rstd[:, NG:NG + 1], 0.0)
            dve.memset(nmr[:, NG:NG + 1], 0.0)
            dve.wait_ge(ld_x[0], 16)
            moments(0, 0).then_inc(gn_stats, 1)
            chain(dve.memset(vsb[:], 0.0))
            dve.memset(vsb[0:WT, :, :, 8:9], 1.0)
            dve.memset(vsb[64:WP, :, :, 17:18], 1.0).then_inc(init_dve, 1)
            variances(0, 1, 1, bk[2])
            dve.wait_ge(ld_w, 16)
            dve.tensor_scalar(bqs[:], ww("bq"), SCALE, None, ALU.mult).then_inc(bqs_ready, 1)
            shifts(0, 1, 1)
            dve.wait_ge(gn_ready, 1)
            dve.wait_ge(init_pool, 2)

            def normalise(g, R, r):
                if not (isinstance(R, int) and R < 2):
                    dve.wait_ge(v_done, R - 1)
                for a, b, s, c, e, t in pieces(r):
                    whole = (e - c) // WS if c == 0 else 0
                    runs = [(c, whole, WS)] if whole else []
                    runs.append((c + whole * WS, 1, e - c - whole * WS))
                    for c0, n, m in runs:
                        t0 = t + c0 - c
                        last = dve.tensor_scalar(
                            xn[:, r % 2, c0 // WS:c0 // WS + n, 0:WT].rearrange("p n (i j) -> p n i j", i=WS)
                            [:, :, a:b, c0 % WS:c0 % WS + m],
                            x[:, g, s:s + b - a, t0:t0 + n * m].rearrange("p i (n j) -> p n i j", n=n),
                            rstd[:, bass.ds(g, 1)], nmr[:, bass.ds(g, 1)], ALU.mult, ALU.add)
                last.then_inc(xn_half, 1)
                dve.wait_ge(xn_half, R + 1)
                dve.tensor_copy(xn[:, r % 2, :, 64:WP], xn[:, r % 2, :, 0:WT]).then_inc(xn_ready, 1)

            def shift(W, s):
                dve.wait_ge(s_done, W + 1)
                sc = ps_s[s][0:WP, 0:NH * WT].rearrange("p (h k) -> p h k", k=WT)
                dve.tensor_reduce(mx[0:WP, s], sc, AXX, ALU.max).then_inc(max_done, 1)
                dve.wait_ge(max_done, W + 1)
                if not (isinstance(W, int) and W < 2):
                    dve.wait_ge(t_done, W - 1)
                dve.tensor_tensor(d[0:WP, s, :, 0:WT], sc,
                                  mx[0:WP, s].rearrange("p (h o) -> p h o", o=1).broadcast_to([WP, NH, WT]),
                                  ALU.subtract).then_inc(sub_done, 1)

            def weigh(R, b):
                dve.wait_ge(pv_done, NW * R + 2 * b + 2)
                o = ps_o[b][:, 0:288].rearrange("p (a w h e) -> p a w h e", a=2, w=2, e=9)
                for w in range(2):
                    q = slice(64 * w, 64 * w + WT)
                    last = dve.reciprocal(rc[q], o[q, :, w, :, 8])
                last.then_inc(rc_done, 1)
                dve.wait_ge(rc_done, 2 * R + b + 1)
                if b == 0 and not (isinstance(R, int) and R == 0):
                    dve.wait_ge(ot_done, R)
                for w in range(2):
                    q = slice(64 * w, 64 * w + WT)
                    last = dve.tensor_tensor(
                        osb[q, 2 * b:2 * b + 2, :].rearrange("p a (h e) -> p a h e", e=HD), o[q, :, w, :, 0:HD],
                        rc[q].rearrange("p a (h o) -> p a h o", o=1).broadcast_to([WT, 2, NH, HD]), ALU.mult)
                last.then_inc(o_ready, 1)

            def residual(g, R, r):
                dve.wait_ge(proj_done, R + 1)
                y = ps_x[:, 0:RT].rearrange("p (i j) -> p i j", j=HW)
                for a, b, s, c, e, t in pieces(r):
                    xx = x[:, g, s:s + b - a, t:t + e - c]
                    last = dve.scalar_tensor_tensor(out=xx, in0=y[:, a:b, c:e], scalar=bt[:, 0:1], in1=xx,
                                                    op0=ALU.add, op1=ALU.add)
                last.then_inc(res_done, 1)

            normalise(0, 0, 0)
            normalise(0, 1, 1)
            dve.memset(pt[:], 0.0)
            dve.memset(d[:], 0.0).then_inc(init_dve, 1)
            dve.wait_ge(pe_bt, 1)
            dve.tensor_tensor(bt[:], bk[3][:, 0:1], ww("bp"), ALU.add).then_inc(bt_ready, 1)
            dve.wait_ge(bt_ready, 1)
            dve.wait_ge(init_pool, 5)
            dve.wait_ge(init_dve, 2)
            shift(0, 0)

            def kernel_sums():
                dve.wait_ge(ld_k1, 16)
                k1f = ker1[:].rearrange("p t c -> p (t c)")
                h1f = h1[:, 0].rearrange("p a b -> p (a b)")[:, 0:NTAP * C]
                chain(dve.scalar_tensor_tensor(out=h1f, in0=k1f, scalar=-1.0, in1=k1f, op0=ALU.mult, op1=ALU.max))
                dve.tensor_reduce(asum[:], h1f.rearrange("p (t c) -> p c t", c=C), AXX, ALU.add)\
                   .then_inc(asum_ready, 1)

            def kernel_signs(n):
                dve.wait_ge(init_pool, 6)
                for w in range(2):
                    q = slice(64 * w, 64 * w + 64)
                    if n == 0:
                        last = dve.tensor_scalar(w1[q, :, 64 * w:64 * w + 64], ker1[q], 0.0, 0.5, ALU.is_gt,
                                                 ALU.subtract)
                    else:
                        dve.wait_ge(ld_k2, 16)
                        blk = w2[q, :, 64 * w:64 * w + 64]
                        chain(dve.tensor_scalar(blk, ker2[q], 0.0, None, ALU.is_lt))
                        last = dve.scalar_tensor_tensor(out=blk, in0=ker2[q], scalar=0.0, in1=blk, op0=ALU.is_gt,
                                                        op1=ALU.subtract)
                last.then_inc((w1_ready, w2_ready)[n], 1)

            def tap_weights():
                dve.wait_ge(ld_late, 16)
                for n in range(2):
                    last = dve.tensor_tensor(g12[:, n, :], ww("wx"), ww("cw")[:, n * P:(n + 1) * P], ALU.mult)
                last.then_inc(g12_ready, 1)

            def body(g, first):
                for r in range(NW):
                    R = g * NW + r
                    W = g * NWIN + r * NW
                    if r == 1 and not first:
                        dve.wait_ge(res_done, R - 1)
                    shift(W + 1, 1)
                    if first and r == 1:
                        variances(1, NG - 1, 2, ps_qk)
                    if first and r == 2:
                        dve.wait_ge(gn_ready, 2)
                    normalise(g if r < 2 else g + 1, R + 2, (r + 2) % NW)
                    if not (first and r == 0):
                        weigh(R - 1, 1)
                    shift(W + 2, 0)
                    if first and r == 0:
                        for n in range(1, NG):
                            dve.wait_ge(ld_x[n], 16)
                            last = moments(n, 0)
                        last.then_inc(gn_stats, 1)
                    shift(W + 3, 1)
                    if first and r == 1:
                        kernel_sums()
                    if first and r == 2:
                        kernel_signs(0)
                    if first and r == 3:
                        kernel_signs(1)
                        tap_weights()
                    weigh(R, 0)
                    shift(W + 4, 0)
                    if not (first and r == 0):
                        residual(g if r else g - 1, R - 1, (r - 1) % NW)
                    if r == 1:
                        if first:
                            shifts(1, NG - 1, 2)
                        else:
                            half_moments(g - 1)

            body(0, True)
            with dve.Fori(1, NG) as g:
                body(g, False)

            def signs(g):
                if g == 0:
                    dve.wait_ge(init_pool, 7)
                dve.wait_ge(gn_copied, 3 if g < NG - 1 else 4)
                if g >= 2:
                    dve.wait_ge(conv_done, 2 * (g - 1))
                dve.tensor_scalar(sg1[:, g % 2, 1:1 + HW, 1:1 + HW], x[:, g], sg[:, col(1, g), 0:1], 0.5,
                                  ALU.is_gt, ALU.subtract).then_inc(sg_ready, 1)

            def finish1(g):
                for i in range(2):
                    u = 2 * g + i
                    xx = xflat[:, g, i * HALF:(i + 1) * HALF]
                    dve.wait_ge(conv_done, u + 1)
                    dve.wait_ge(ka_ready, u + 1)
                    dve.tensor_tensor(prod[:, i], bk[u % 4][:, 0:HALF], ka[:, i], ALU.mult).then_inc(prod_done, 1)
                    dve.wait_ge(prod_done, u + 1)
                    dve.scalar_tensor_tensor(out=xx, in0=prod[:, i], scalar=ww("b1"), in1=xx, op0=ALU.add,
                                             op1=ALU.add).then_inc(x_done, 1)
                dve.wait_ge(x_done, 2 * g + 2)
                moments(g, 2).then_inc(gn_stats, 1)

            def remainder(g):
                s = g % 2
                dve.wait_ge(p1_ready, g + 1)
                if g >= 2:
                    dve.wait_ge(p2_ready, g - 1)
                dve.tensor_tensor(rem[:, s], xf[:, s], parts[:, s, 0, 1:1 + HW, 1:1 + HW], ALU.subtract)\
                   .then_inc(rem_ready, 1)

            def third(g):
                s = g % 2
                dve.wait_ge(rem_ready, g + 1)
                dve.wait_ge(p2_ready, g + 1)
                dve.tensor_tensor(parts[:, s, 2, 1:1 + HW, 1:1 + HW], rem[:, s], parts[:, s, 1, 1:1 + HW, 1:1 + HW],
                                  ALU.subtract).then_inc(p3_ready, 1)

            def finish2(g):
                for i in range(2):
                    u = 2 * NG + 2 * g + i
                    xx = xflat[:, g, i * HALF:(i + 1) * HALF]
                    dve.wait_ge(conv_done, u + 1)
                    dve.tensor_tensor(xx, bk[u % 4][:, 0:HALF], xx, ALU.add).then_inc(x_done, 1)
                dve.wait_ge(x_done, 2 * NG + 2 * g + 2)
                moments(g, 3).then_inc(gn_stats, 1)

            def gate(v):
                for w in range(2):
                    u = 2 * v + w
                    dve.wait_ge(su_ready, u + 1)
                    dve.wait_ge(sz_ready, u + 1)
                    if v >= 2:
                        dve.wait_ge(out_done, v - 1)
                    dve.scalar_tensor_tensor(out=yy[:, 2 * (v % 2) + w, :], in0=su[:, u % 2], scalar=4.0,
                                             in1=sz[:, u % 2], op0=ALU.mult, op1=ALU.mult).then_inc(y_ready, 1)

            def result(v):
                g, i = v // 2, v % 2
                dve.wait_ge(out_done, v + 1)
                dve.tensor_tensor(res[:, g, i * HALF:(i + 1) * HALF], bk[4 + v % 2][:, 0:HALF],
                                  xflat[:, g, i * HALF:(i + 1) * HALF], ALU.add).then_inc(res_ready, 1)

            for g in range(NG - 1):
                last = merge(g, col(1, g), NG + NG - 1)
            last.then_inc(gn_stats, 1)
            weigh(NG * NW - 1, 1)
            variances(col(1, 0), NG - 1, 3, ps_qk)
            signs(0)
            shifts(col(1, 0), NG - 1, 3)
            dve.wait_ge(pe_alpha, 1)
            for w in range(2):
                q = slice(64 * w, 64 * w + 64)
                last = dve.tensor_scalar(aw[q, 64 * w:64 * w + 64], ps_qk[q, C:2 * C],
                                         4.0 / (NTAP * C) / (NTAP * C), None, ALU.mult)
            last.then_inc(aw_ready, 1)
            signs(1)
            residual(NG - 1, NG * NW - 1, NW - 1)
            dve.wait_ge(res_done, NG * NW)
            moments(NG - 1, 1).then_inc(gn_stats, 1)
            signs(2)
            finish1(0)
            variances(col(1, NG - 1), 1, 4, bk[7])
            signs(3)
            finish1(1)
            shifts(col(1, NG - 1), 1, 4)
            variances(col(2, 0), 1, 5, bk[7])
            finish1(2)
            shifts(col(2, 0), 1, 5)
            variances(col(2, 1), 1, 6, bk[7])
            finish1(3)
            remainder(0)
            shifts(col(2, 1), 1, 6)
            variances(col(2, 2), 1, 7, bk[7])
            third(0)
            remainder(1)
            shifts(col(2, 2), 1, 7)
            third(1)
            variances(col(2, 3), 1, 8, bk[7])
            shifts(col(2, 3), 1, 8)
            finish2(0)
            remainder(2)
            third(2)
            variances(col(3, 0), 1, 9, bk[7])
            shifts(col(3, 0), 1, 9)
            finish2(1)
            remainder(3)
            third(3)
            variances(col(3, 1), 1, 10, bk[7])
            shifts(col(3, 1), 1, 10)
            finish2(2)
            variances(col(3, 2), 1, 11, bk[7])
            shifts(col(3, 2), 1, 11)
            finish2(3)
            for v in range(2 * NG):
                gate(v)
                if v >= 1:
                    result(v - 1)
                if v == 1:
                    variances(col(3, 3), 1, 12, bk[7])
                    shifts(col(3, 3), 1, 12)
            result(2 * NG - 1)


def pair(a):
    n = a.shape[1]
    o = np.zeros((P, 2, n), a.dtype)
    o[:C, 0] = a
    o[C:, 1] = a
    return o


def constants():
    c = np.zeros((P, NCI), np.float32)
    i = np.arange(P)
    c[i, CI["ident"][0] + i] = 1
    for o, s in ((0, 0.5), (1, 0.5)):
        c[i, CI["avg"][0] + (i ^ o)] = 0.5
    c[i, CI["diff"][0] + i] = 0.5
    c[i, CI["diff"][0] + (i ^ 1)] = -0.5
    c[:C, CI["ones"][0]:CI["ones"][0] + C] = 1
    c[C:, CI["ones"][0] + C:CI["ones"][0] + P] = 1
    c[i, CI["kmask"][0] + (i % 32) // HD] = 1
    late = (np.arange(WS) >= WS - SH).astype(int)
    row, col = np.repeat(late, WS), np.tile(late, WS)
    regions = [row == 0, row == 1, col == 0, col == 1]
    regions += [(row == a) & (col == b) for a in range(2) for b in range(2)]
    qfix = np.zeros((NW, 64, NW, P), np.float32)
    q = np.arange(WT)
    for r in range(NW):
        for a in range(NW):
            use = {(0, 0): [], (1, 0): [0, 1], (0, 1): [2, 3], (1, 1): [4, 5, 6, 7]}[(r == NW - 1, a == NW - 1)]
            for w in range(2):
                qfix[r, q, a, 64 * w + q] = 1
                for k in use:
                    qfix[r, WT + k, a, 64 * w:64 * w + WT] = regions[k]
    return c, qfix, np.array(regions)


def kernel(x, L0_conv_qkv_weight, L0_conv_qkv_bias, L0_conv_proj_weight, L0_conv_proj_bias,
           L0_conv_relative_position_bias, L1_conv_kernel, L1_conv_bias, L2_conv_kernel, L3_conv_W_in,
           L3_conv_conv_w, L3_conv_conv_b, L3_conv_W_out):
    import concourse.bacc as bacc
    from concourse.bass_utils import run_bass_kernel_spmd

    f = np.float32
    x = np.asarray(x)
    wqkv, bqkv = np.asarray(L0_conv_qkv_weight), np.asarray(L0_conv_qkv_bias)
    wp, bp = np.asarray(L0_conv_proj_weight), np.asarray(L0_conv_proj_bias)
    rel = np.asarray(L0_conv_relative_position_bias)
    k1, b1 = np.asarray(L1_conv_kernel), np.asarray(L1_conv_bias)
    k2 = np.asarray(L2_conv_kernel)
    win, cw, cb, wo = (np.asarray(a) for a in (L3_conv_W_in, L3_conv_conv_w, L3_conv_conv_b, L3_conv_W_out))

    cst, qfix, regions = constants()
    kfix = np.zeros((2, 64, 4, NW, WT), f)
    for j in range(2):
        kfix[j, 0:WT] = rel[0, 4 * j:4 * j + 4].transpose(1, 0, 2)[:, :, None, :]
        for k, reg in enumerate(regions):
            kfix[j, WT + k] = np.where(reg, 0, -100)

    w = [np.zeros((P, n), f) for n in WIDTHS]

    def put(name, a):
        t, at, n = WI[name]
        w[t][:, at:at + n] = a.reshape(P, n)

    def by_head_half(a):
        return a.reshape(-1, 2, 2, 32).transpose(0, 2, 1, 3).reshape(-1, P)

    both = lambda v: np.concatenate([v, v])
    put("wq", by_head_half(pair(wqkv[0:C].T)))
    put("wk", by_head_half(pair(wqkv[C:2 * C].T)))
    wv = pair(wqkv[2 * C:].T).reshape(P, 2, 4, 2, HD)
    put("wv", wv.transpose(0, 3, 2, 1, 4))
    put("wp", pair(wp.T))
    put("bq", by_head_half(both(bqkv[0:C])[None]))
    put("bk", by_head_half(both(bqkv[C:2 * C])[None]))
    put("bv", both(bqkv[2 * C:]))
    put("bp", both(bp))
    put("b1", both(b1))
    put("cb", cb)
    put("wx", both(win[0:DI].T))
    put("wz", both(win[DI:].T))
    cwt = cw[:, 0, :].T
    put("cw", np.concatenate([np.repeat(cwt[None, [3, 1]], C, 0), np.repeat(cwt[None, [2, 0]], C, 0)]))
    put("wo", wo.T)
    taps = lambda k: np.ascontiguousarray(both(k.reshape(NTAP, C, C).transpose(1, 0, 2)))

    arrays = {
        "x_in": np.ascontiguousarray(x.reshape(NG, 2, TOK, C).transpose(1, 3, 0, 2).reshape(P, NG, TOK)),
        "cst_in": cst, "wts_in": w[0], "late_in": w[1], "ker1_in": taps(k1), "ker2_in": taps(k2), "qfix_in": qfix,
        "kfix_in": kfix.reshape(2, 64, 4, RT),
    }
    nc = bacc.Bacc("TRN2", target_bir_lowering=False, num_devices=1)
    args = [nc.dram_tensor(n, a.shape, mybir.dt.from_np(a.dtype), kind="ExternalInput").ap()
            for n, a in arrays.items()]
    args.append(nc.dram_tensor("out", (P, NG, TOK), F32, kind="ExternalOutput").ap())
    program(nc, *args)
    r = run_bass_kernel_spmd(nc, [arrays], core_ids=[0])
    y = np.asarray(r.results[0]["out"]).reshape(2, C, NG, HW, HW)
    return np.ascontiguousarray(y.transpose(2, 0, 3, 4, 1).reshape(2 * NG, HW, HW, C))
```

```python
from contextlib import ExitStack

import numpy as np

import concourse.bass as bass
from concourse import mybir

ALU = mybir.AluOpType
ACT = mybir.ActivationFunctionType
AXX = mybir.AxisListType.X
F32 = mybir.dt.float32
BF16 = mybir.dt.bfloat16

P = 128
C = 64
HW = 28
TOK = HW * HW
NG = 4
WS = 7
SH = 3
NW = HW // WS
WT = WS * WS
RT = NW * WT
NH = 8
HD = C // NH
NWIN = NW * NW
WQ = 2 * WT
WK = 64 + WT
HALF = TOK // 2
HR = HW // 2
PAD = HW + 2
NTAP = 9
DI = 2 * C
EPS = 1e-5
SCALE = HD ** -0.5

CI = dict(ident=(0, P), avg=(P, P), diff=(2 * P, P), ones=(3 * P, P), kmask=(4 * P, 4))
NCI = 4 * P + 4
WI, WIDTHS = {}, []
for part_ in ((("wq", P), ("wk", P), ("wv", P), ("wp", P), ("bq", 1), ("bk", 1), ("bv", 1), ("bp", 1)),
              (("b1", 1), ("cb", 1), ("wx", P), ("wz", P), ("cw", 4 * P), ("wo", C))):
    at_ = 0
    for name_, n_ in part_:
        WI[name_] = (len(WIDTHS), at_, n_)
        at_ += n_
    WIDTHS.append(at_)


def program(nc, x_in, cst_in, wts_in, late_in, ker1_in, ker2_in, qfix_in, kfix_in, out):
    ctx = ExitStack()
    with ctx:
        def sb(name, shape, dt=F32):
            return ctx.enter_context(nc.sbuf_tensor(name, shape, dt))

        def bank(name):
            return ctx.enter_context(nc.psum_tensor(name, [P, 512], F32))

        def sem(name):
            return ctx.enter_context(nc.semaphore(name))

        x = sb("x", [P, NG + 1, HW, HW])
        cst = sb("cst", [P, NCI])
        wts = sb("wts", [P, WIDTHS[0]])
        late = sb("late", [P, WIDTHS[1]])
        ker1 = sb("ker1", [P, NTAP, C])
        ker2 = sb("ker2", [P, NTAP, C])

        def cc(name):
            a, n = CI[name]
            return cst[:, a:a + n]

        def ww(name):
            t, a, n = WI[name]
            return (wts, late)[t][:, a:a + n]

        xn = sb("xn", [P, 2, NW, WT])
        qbd = sb("qbd", [P, NW, 2, NW, WQ])
        ks = sb("ks", [P, RT])
        kex = sb("kex", [P, 2, 2, 4, RT])
        d = sb("d", [P, 2, NH, 64])
        mx = sb("mx", [P, 2, NH])
        pt = sb("pt", [P, 2, NH // 2, WQ])
        vsb = sb("vsb", [P, 2, NW * 4 * 2, 18])
        rc = sb("rc", [P, 2, NH])
        osb = sb("osb", [P, NW, C])
        att = sb("att", [P, NW, WS, WS])
        bqs = sb("bqs", [P, 1])
        bt = sb("bt", [P, 1])
        NJ = 4 * (NG + 1)

        def col(l, g):
            return l * (NG + 1) + g

        def nth(l, g):
            return 3 + NG * (l - 1) + g + 1 if l else min(g, 2) + 1

        warm = sb("warm", [P, 1])
        st = sb("st", [P, 2, 2, 6])
        mv = sb("mv", [P, NJ, 2])
        sg = sb("sg", [P, NJ, 3])
        ve = sb("ve", [P, NJ])
        mhalf = sb("mhalf", [P, NG])
        rstd = sb("rstd", [P, NJ])
        nmr = sb("nmr", [P, NJ])
        w1 = sb("w1", [P, NTAP, P], BF16)
        asum = sb("asum", [P, C])
        aw = sb("aw", [P, P])
        sg1 = sb("sg1", [P, NG, PAD, PAD], BF16)
        ab = sb("ab", [P, PAD, PAD])
        h1 = sb("h1", [P, PAD, HW])
        h2 = sb("h2", [P, PAD, HW])
        v1 = sb("v1", [P, HW, HW])
        v2 = sb("v2", [P, NG, HW, HW])
        ka = sb("ka", [P, 2, HALF])
        prod = sb("prod", [P, 2, HALF])
        w2 = sb("w2", [P, NTAP, C], BF16)
        parts = sb("parts", [P, 2, 3, PAD, PAD], BF16)
        p12 = sb("p12", [P, 2, 2, PAD, PAD], BF16)
        p33 = sb("p33", [P, 2, 2, PAD, PAD], BF16)
        w2b = sb("w2b", [P, 3, C], BF16)
        xf = sb("xf", [P, 2, HW, HW])
        rem = sb("rem", [P, 2, HW, HW])
        SHF = 3
        g12 = sb("g12", [P, 2, 2, P])
        xs = sb("xs", [P, 2, 2, SHF + TOK])
        su = sb("su", [P, 2, HALF])
        sz = sb("sz", [P, 2, HALF])
        yy = sb("yy", [P, 4, HALF])
        res = sb("res", [P, NG, TOK])

        bk = [bank(f"bank{i}") for i in range(8)]
        ps_s, ps_t, ps_o = bk[0:2], bk[2:4], bk[4:6]
        ps_qk, ps_x = bk[6], bk[7]

        def sems(names):
            return [sem(n) for n in names.split()]

        ld_x0, ld_x1, ld_c, ld_w, ld_late, ld_k1, ld_k2, ld_fix0, ld_fix = sems(
            "ld_x0 ld_x1 ld_c ld_w ld_late ld_k1 ld_k2 ld_fix0 ld_fix")
        warm_set, vsb_zeroed, init_dve, init_pool = sems("warm_set vsb_zeroed init_dve init_pool")
        bqs_ready, pe_bt, bt_ready, kabs_ready, asum_ready, pe_alpha = sems(
            "bqs_ready pe_bt bt_ready kabs_ready asum_ready pe_alpha")
        w1_ready, w2_ready, aw_ready, g12_ready = sems("w1_ready w2_ready aw_ready g12_ready")
        bn_done, gn_stats, gn_mixed, gn_copied, gn_square, gn_var, gn_rstd, gn_ready = sems(
            "bn_done gn_stats gn_mixed gn_copied gn_square gn_var gn_rstd gn_ready")
        xn_ready, qk_done, q_ready, ks_ready, kex_ready, v_done, v_ready = sems(
            "xn_ready qk_done q_ready ks_ready kex_ready v_done v_ready")
        rc_done, o_ready, ot_done, att_ready, proj_done, res_done = sems(
            "rc_done o_ready ot_done att_ready proj_done res_done")
        s_done, max_done, sub_done, t_done, exp_done, pv_done = sems("s_done max_done sub_done t_done exp_done pv_done")
        sg_ready, ab_ready, h1_done, h_done, v1_done, box_ready = sems(
            "sg_ready ab_ready h1_done h_done v1_done box_ready")
        conv_done, ka_done, ka_ready, prod_done, x_done = sems("conv_done ka_done ka_ready prod_done x_done")
        p1_ready, rem_ready, p2_ready, p2_placed, p3_ready = sems("p1_ready rem_ready p2_ready p2_placed p3_ready")
        stacked, thirds_stacked = sems("stacked0 stacked1"), sems("thirds_stacked0 thirds_stacked1")
        xs_ready, xs_back_ready, u_done, z_done, su_ready, sz_ready, y_ready, out_done, res_ready, stored = sems(
            "xs_ready xs_back_ready u_done z_done su_ready sz_ready y_ready out_done res_ready stored")

        def pieces(r):
            rows = [(0, WS, WS * r + SH)] if r < NW - 1 else [(0, WS - SH, HW - (WS - SH)), (WS - SH, WS, 0)]
            cols = [(0, HW - SH, SH), (HW - SH, HW, 0)]
            return [(a, b, s, c, e, t) for a, b, s in rows for c, e, t in cols]

        xflat = x[:].rearrange("p g h w -> p g (h w)")

        def mask_half(engine, par, j):
            q = slice(64 * j, 64 * j + 64)
            engine.tensor_tensor(
                kex[q, par, j], ks[q, :].rearrange("p (o t) -> p o t", o=1).broadcast_to([64, 4, RT]),
                cc("kmask")[q, :].rearrange("p (a o) -> p a o", o=1).broadcast_to([64, 4, RT]), ALU.mult)\
                .then_inc(kex_ready, 1)

        def third_part(engine, g):
            s = g % 2
            engine.wait_ge(rem_ready, g + 1)
            engine.wait_ge(p2_ready, g + 1)
            if g >= 2:
                engine.wait_ge(conv_done, 2 * NG + 2 * (g - 1))
            engine.tensor_tensor(parts[:, s, 2, 1:1 + HW, 1:1 + HW], rem[:, s], parts[:, s, 1, 1:1 + HW, 1:1 + HW],
                                 ALU.subtract).then_inc(p3_ready, 1)

        def stacked_by(g):
            return 16 * (4 * (g // 2 + 1) - (2 if g % 2 == 0 else 0))

        block = ctx.enter_context(nc.Block())

        @block.sync
        def _(sp):
            sp.dma_start(xflat[:, 0, :], x_in[:, 0, :]).then_inc(ld_x0, 16)
            sp.dma_start(wts[:], wts_in).then_inc(ld_w, 16)

            def fixed(j):
                return slice(64 * (1 - j), 64 * (2 - j))

            for j in range(2):
                sp.dma_start(kex[fixed(j), 0, j], kfix_in[j]).then_inc(ld_fix0, 16)
                sp.dma_start(qbd[fixed(j), 0, j], qfix_in[:, 0]).then_inc(ld_fix0, 16)
            for j in range(2):
                sp.dma_start(kex[fixed(j), 1, j], kfix_in[j]).then_inc(ld_fix, 16)
                sp.dma_start(qbd[fixed(j), 1:NW, j], qfix_in[:, 1:NW]).then_inc(ld_fix, 16)
            sp.dma_start(xflat[:, 1:NG, :], x_in[:, 1:NG, :]).then_inc(ld_x1, 16)
            sp.dma_start(ker1[:], ker1_in).then_inc(ld_k1, 16)
            sp.dma_start(ker2[:], ker2_in).then_inc(ld_k2, 16)
            sp.dma_start(late[:], late_in).then_inc(ld_late, 16)
            for g in range(NG):
                s = g % 2
                if g >= 2:
                    sp.wait_ge(conv_done, 2 * NG + 2 * (g - 1))
                for part, signal in enumerate((p1_ready, p2_ready)):
                    if part == 0 or g > 0:
                        sp.wait_ge(signal, g + 1)
                        for w in range(2):
                            sp.dma_start(p12[64 * part:64 * part + 64, s, w],
                                         parts[64 * w:64 * w + 64, s, part]).then_inc(stacked[s], 16)
                if g > 0:
                    sp.wait_ge(p3_ready, g + 1)
                    for row in range(2):
                        for w in range(2):
                            sp.dma_start(p33[64 * row:64 * row + 64, s, w, 0:PAD - row],
                                         parts[64 * w:64 * w + 64, s, 2, row:PAD]).then_inc(thirds_stacked[s], 16)
            for g in range(NG):
                for i in range(2):
                    sp.wait_ge(res_ready, 2 * g + i + 1)
                    sp.dma_start(out[:, g, i * HALF:(i + 1) * HALF],
                                 res[:, g, i * HALF:(i + 1) * HALF]).then_inc(stored, 16)
            sp.wait_ge(stored, 16 * 2 * NG)

        @block.gpsimd
        def _(pool):
            pool.memset(mhalf[:], -0.5).then_inc(init_pool, 1)
            pool.wait_ge(init_pool, 1)
            pool.memset(qbd[0:64, :, 0], 0.0).then_inc(init_pool, 1)
            pool.wait_ge(init_pool, 2)
            pool.memset(qbd[64:P, :, 1], 0.0).then_inc(init_pool, 1)

            def rsqrt(j, n, count):
                pool.wait_ge(gn_var, count)
                pool.tensor_tensor(rstd[:, bass.ds(j, n)], ve[:, bass.ds(j, n)], mhalf[:, 0:n], ALU.pow)\
                    .then_inc(gn_rstd, 1)

            pool.wait_ge(init_pool, 3)
            rsqrt(0, 1, 1)
            pool.wait_ge(ld_c, 16)
            pool.wait_ge(gn_rstd, 1)

            def mask_keys(R, par):
                pool.wait_ge(ks_ready, R + 1)
                for j in range(2):
                    pool.wait_ge(kex_ready, R + R + j)
                    mask_half(pool, par, j)

            pool.wait_ge(ks_ready, 1)
            mask_half(pool, 0, 0)
            mask_keys(1, 1)

            def row_sums(n):
                pool.wait_ge(ab_ready, n)
                pool.tensor_tensor(h1[:], ab[:, :, 0:HW], ab[:, :, 1:HW + 1], ALU.add).then_inc(h1_done, 1)
                pool.wait_ge(h1_done, n)
                pool.tensor_tensor(h2[:], h1[:], ab[:, :, 2:PAD], ALU.add).then_inc(h_done, 1)
                pool.wait_ge(h_done, n)

            def box_sums(p, n):
                pool.tensor_tensor(v1[:], h2[:, 0:HW], h2[:, 1:HW + 1], ALU.add).then_inc(v1_done, 1)
                pool.wait_ge(v1_done, n)
                pool.tensor_tensor(v2[:, bass.ds(p, 1)].rearrange("p o a b -> p (o a) b"), v1[:], h2[:, 2:PAD],
                                   ALU.add).then_inc(box_ready, 1)

            def binary_signs():
                pool.wait_ge(ld_k1, 16)
                for w in range(2):
                    q = slice(64 * w, 64 * w + 64)
                    pool.tensor_scalar(w1[q, :, 64 * w:64 * w + 64], ker1[q], 0.0, 0.5, ALU.is_gt, ALU.subtract)\
                        .then_inc(w1_ready, 1)
                    pool.wait_ge(w1_ready, w + 1)

            def ternary_signs():
                pool.wait_ge(ld_k2, 16)
                above = p33[:, 0, 0].rearrange("p a b -> p (a b)")[:, 0:NTAP * C].rearrange("p (t c) -> p t c", c=C)
                pool.tensor_scalar(above, ker2[:], 0.0, None, ALU.is_gt)
                pool.tensor_scalar(w2[:], ker2[:], 0.0, None, ALU.is_lt).then_inc(w2_ready, 1)
                pool.wait_ge(w2_ready, 1)
                pool.tensor_tensor(w2[:], above, w2[:], ALU.subtract).then_inc(w2_ready, 1)
                pool.wait_ge(w2_ready, 2)
                for ky in range(2):
                    q = slice(64 * ky, 64 * ky + 64)
                    pool.tensor_copy(w2b[q], w2[q, 3 * ky:3 * ky + 3]).then_inc(w2_ready, 1)
                    pool.wait_ge(w2_ready, 3 + ky)

            def border(t, value):
                pool.memset(t[..., ::PAD - 1, :], value)
                return pool.memset(t[..., 1:PAD - 1, ::PAD - 1], value)

            def body(g, first):
                for r in range(NW):
                    R = g * NW + r
                    if r == 2 and not first:
                        pool.wait_ge(kex_ready, 2 * R + 4)
                        rsqrt(col(1, 0), 1, nth(1, g - 1))
                        pool.wait_ge(gn_rstd, nth(1, g - 1))
                    if r == 3 and not first:
                        pool.wait_ge(kex_ready, 2 * R + 4)
                        row_sums(g)
                    if r == 3 and first:
                        pool.wait_ge(kex_ready, 2 * R + 4)
                        rsqrt(2, 2, 3)
                        pool.wait_ge(gn_rstd, 3)
                    mask_keys(R + 2, r % 2)
                    if first:
                        pool.wait_ge(kex_ready, 2 * R + 6)
                    if first and r == 0:
                        pool.memset(w1[:], 0.0)
                        pool.memset(aw[:], 0.0).then_inc(init_pool, 1)
                        border(ab, 0.0)
                        border(sg1, -0.5)
                        border(parts, 0.0)
                        border(p12[:, 0], 0.0)
                        pool.memset(xs[:, :, :, 0:SHF + 1], 0.0).then_inc(init_pool, 1)
                        pool.wait_ge(init_pool, 5)
                    if first and r == 1:
                        rsqrt(1, 1, 2)
                        pool.wait_ge(gn_rstd, 2)
                        binary_signs()
                    if first and r == 2:
                        ternary_signs()
                    if r == 3 and not first:
                        pool.wait_ge(kex_ready, 2 * R + 6)
                        box_sums(g - 1, g)
                        pool.wait_ge(box_ready, g)

            body(0, True)
            with pool.Fori(1, NG) as g:
                body(g, False)
            pool.wait_ge(kex_ready, 2 * NG * NW + 4)
            rsqrt(col(1, NG - 1), 1, nth(1, NG - 1))
            rsqrt(col(2, 0), 1, nth(2, 0))
            row_sums(NG)
            rsqrt(col(2, 1), 1, nth(2, 1))
            box_sums(NG - 1, NG)
            rsqrt(col(2, 2), 1, nth(2, 2))
            third_part(pool, 1)
            rsqrt(col(2, 3), 1, nth(2, 3))
            third_part(pool, 2)
            third_part(pool, 3)
            for g in range(NG):
                rsqrt(col(3, g), 1, nth(3, g))

        @block.scalar
        def _(act):
            act.dma_start(cst[:], cst_in).then_inc(ld_c, 16)
            act.wait_ge(warm_set, 1)
            act.activation(warm[:], warm[:], ACT.Exp).then_inc(warm_set, 1)

            def evac_qk(R, r):
                act.wait_ge(qk_done, R + 1)
                if not (isinstance(R, int) and R == 0):
                    act.wait_ge(kex_ready, 2 * R)
                act.activation(ks[:], ps_qk[:, RT:2 * RT], ACT.Identity, bias=ww("bk")).then_inc(ks_ready, 1)
                for j in range(2):
                    for w in range(2):
                        q = slice(64 * j + 32 * w, 64 * j + 32 * w + 32)
                        last = act.activation(qbd[q, r, j, :, WT * w:WT * w + WT],
                                              ps_qk[q, 0:RT].rearrange("p (a t) -> p a t", a=NW),
                                              ACT.Identity, bias=bqs[q, 0:1], scale=SCALE)
                last.then_inc(q_ready, 1)

            def evac_v(R, par):
                act.wait_ge(v_done, R + 1)
                if not (isinstance(R, int) and R < 2):
                    act.wait_ge(pv_done, R * NW - NW)
                for e in range(2):
                    q = slice(64 * e, 64 * e + WT)
                    last = act.activation(vsb[q, par].rearrange("p (a n) d -> p a n d", a=NW)
                                          [:, :, :, 9 * e:9 * e + HD],
                                          ps_x[q, 0:NW * C].rearrange("p (a n d) -> p a n d", a=NW, d=HD),
                                          ACT.Identity)
                last.then_inc(v_ready, 1)

            def expo(W, s):
                act.wait_ge(t_done, W + 1)
                if not (isinstance(W, int) and W < 2):
                    act.wait_ge(pv_done, W - 1)
                act.activation(pt[0:WK, s], ps_t[s][0:WK, :].rearrange("p (n t) -> p n t", t=P)[:, :, 0:WQ],
                               ACT.Exp).then_inc(exp_done, 1)

            def evac_att(R):
                act.wait_ge(ot_done, R + 1)
                if not (isinstance(R, int) and R == 0):
                    act.wait_ge(proj_done, R)
                for w in range(2):
                    for b in range(2):
                        last = act.activation(
                            att[64 * w:64 * w + 64, b:NW:2].rearrange("p m i j -> p m (i j)"),
                            ps_x[64 * b:64 * b + 64, 0:2 * P].rearrange("p (m t) -> p m t", t=P)
                            [:, :, 64 * w:64 * w + WT],
                            ACT.Identity)
                last.then_inc(att_ready, 1)

            def absolutes(p, j, n):
                act.wait_ge(gn_ready, nth(1, p))
                if not (isinstance(n, int) and n == 1):
                    act.wait_ge(h_done, n - 1)
                act.activation(ab[:, 1:1 + HW, 1:1 + HW],
                               x[:, bass.ds(p, 1)].rearrange("p o a b -> p (o a) b"), ACT.Abs,
                               bias=nmr[:, j:j + 1], scale=rstd[:, j:j + 1]).then_inc(ab_ready, 1)

            act.wait_ge(ld_w, 16)
            act.wait_ge(bqs_ready, 1)
            act.wait_ge(init_pool, 3)
            evac_qk(0, 0)
            act.wait_ge(init_dve, 1)
            evac_v(0, 0)
            evac_qk(1, 1)

            def body(g, first):
                for r in range(NW):
                    R = g * NW + r
                    W = g * NWIN + r * NW
                    expo(W, 0)
                    evac_v(R + 1, (r + 1) % 2)
                    expo(W + 1, 1)
                    if not (first and r == 0):
                        evac_att(R - 1)
                    evac_qk(R + 2, (r + 2) % NW)
                    expo(W + 2, 0)
                    if first and r == 1:
                        act.wait_ge(ld_k1, 16)
                        act.activation(h1[:].rearrange("p a b -> p (a b)")[:, 0:NTAP * C],
                                       ker1[:].rearrange("p t c -> p (t c)"), ACT.Abs).then_inc(kabs_ready, 1)
                    expo(W + 3, 1)
                    if r == 2 and not first:
                        absolutes(g - 1, col(1, 0), g)

            body(0, True)
            with act.Fori(1, NG) as g:
                body(g, False)
            act.wait_ge(init_pool, 5)

            def evac_ka(u):
                i = u % 2
                act.wait_ge(ka_done, u + 1)
                if u >= 2:
                    act.wait_ge(prod_done, u - 1)
                act.activation(ka[:, i], bk[4 + i][:, 0:HALF], ACT.Identity).then_inc(ka_ready, 1)

            def split_a(g):
                s, j = g % 2, col(2, g)
                act.wait_ge(gn_ready, nth(2, g))
                if g >= 2:
                    act.wait_ge(stacked[s], stacked_by(g - 2))
                    act.wait_ge(p3_ready, g - 1)
                act.activation(xf[:, s], x[:, g], ACT.Identity, bias=nmr[:, j:j + 1], scale=rstd[:, j:j + 1])
                act.activation(parts[:, s, 0, 1:1 + HW, 1:1 + HW], x[:, g], ACT.Identity, bias=nmr[:, j:j + 1],
                               scale=rstd[:, j:j + 1]).then_inc(p1_ready, 1)

            def split_b(g):
                s = g % 2
                act.wait_ge(rem_ready, g + 1)
                if g == 0:
                    for w in range(2):
                        act.activation(p12[64:P, s, w, 1:1 + HW, 1:1 + HW], rem[64 * w:64 * w + 64, s],
                                       ACT.Identity).then_inc(p2_placed, 1)
                act.activation(parts[:, s, 1, 1:1 + HW, 1:1 + HW], rem[:, s], ACT.Identity).then_inc(p2_ready, 1)

            def stack_back(g, w):
                j = col(3, g)
                if w == 0:
                    act.wait_ge(gn_ready, nth(3, g))
                    if g >= 2:
                        act.wait_ge(z_done, 4 * (g - 1))
                q, h = slice(64 * w, 64 * w + 64), slice(64 * (1 - w), 64 * (2 - w))
                act.activation(xs[h, g % 2, w, SHF + 1:SHF + TOK], xflat[q, g, 0:TOK - 1], ACT.Identity,
                               bias=nmr[q, j:j + 1], scale=rstd[q, j:j + 1]).then_inc(xs_back_ready, 1)

            def gates(v, w):
                u = 2 * v + w
                if u >= 2:
                    act.wait_ge(y_ready, u - 1)
                for branch in ("uz", "zu")[w]:
                    if branch == "u":
                        act.wait_ge(u_done, u + 1)
                        act.activation(su[:, w], bk[w][:, 0:HALF], ACT.Silu, bias=ww("cb")).then_inc(su_ready, 1)
                    else:
                        act.wait_ge(z_done, u + 1)
                        act.activation(sz[:, w], bk[2 + w][:, 0:HALF], ACT.Silu).then_inc(sz_ready, 1)

            evac_ka(0)
            evac_att(NG * NW - 1)
            evac_ka(1)
            evac_ka(2)
            evac_ka(3)
            absolutes(NG - 1, col(1, NG - 1), NG)
            split_a(0)
            evac_ka(4)
            evac_ka(5)
            split_b(0)
            split_a(1)
            evac_ka(6)
            split_b(1)
            evac_ka(7)
            for g in range(2, NG):
                split_a(g)
                split_b(g)
            act.wait_ge(ld_late, 16)
            for g in range(2):
                for w in range(2):
                    stack_back(g, w)
            for v in range(2 * NG):
                for w in range(2):
                    gates(v, w)
                    if v in (2, 4):
                        stack_back(v // 2 + 1, w)

        @block.tensor
        def _(pe):
            ident = cc("ident")

            def mix(j, n, count, ps):
                pe.wait_ge(gn_stats, count)
                if not (isinstance(count, int) and count == 1):
                    pe.wait_ge(gn_copied, count - 1)
                pe.matmul(ps[:, 0:2 * n], cc("avg"), mv[:, j:j + n, :].rearrange("p n t -> p (n t)"),
                          start=True, stop=True)
                pe.matmul(ps[:, 2 * n:3 * n], cc("diff"), mv[:, j:j + n, 0], start=True, stop=True)\
                  .then_inc(gn_mixed, 1)

            pe.wait_ge(ld_c, 16)
            mix(0, 1, 1, bk[2])
            pe.wait_ge(ld_w, 16)
            pe.matmul(bk[3][:, 0:1], ww("wp"), ww("bv"), start=True, stop=True).then_inc(pe_bt, 1)

            def proj_qk(R, par, stats=None):
                pe.wait_ge(xn_ready, R + 1)
                if not (isinstance(R, int) and R == 0):
                    pe.wait_ge(q_ready, R)
                    pe.wait_ge(ks_ready, R)
                if isinstance(R, int) and R == 3:
                    pe.wait_ge(gn_copied, 2)
                elif isinstance(R, int) and R == 5:
                    pe.wait_ge(aw_ready, 1)
                    pe.wait_ge(gn_copied, 3)
                elif stats is not None:
                    pe.wait_ge(gn_copied, stats)
                rhs = xn[:, par]
                for n, name in enumerate(("wq", "wk")):
                    mm = pe.matmul(ps_qk[:, n * RT:(n + 1) * RT], ww(name), rhs, start=True, stop=True)
                mm.then_inc(qk_done, 1)

            def proj_v(R, par):
                pe.wait_ge(xn_ready, R + 1)
                if not (isinstance(R, int) and R < 3):
                    pe.wait_ge(res_done, R - 2)
                elif R > 0:
                    pe.wait_ge(v_ready, R)
                for a in range(NW):
                    for e in range(2):
                        mm = pe.matmul(ps_x[64 * e:64 * e + WT, a * C:(a + 1) * C], xn[:, par, a],
                                       ww("wv")[:, e * C:(e + 1) * C], start=True, stop=True)
                mm.then_inc(v_done, 1)

            def scores(W, R, r, par, a):
                s = a % 2
                if a == 0:
                    pe.wait_ge(q_ready, R + 1)
                    pe.wait_ge(kex_ready, 2 * R + 2)
                if not (isinstance(W, int) and W < 2):
                    pe.wait_ge(sub_done, W - 1)
                for j in range(2):
                    mm = pe.matmul(ps_s[s][0:WQ, j * 4 * WT:(j + 1) * 4 * WT], qbd[:, r, j, a],
                                   kex[:, par, j, :, a * WT:(a + 1) * WT], start=True, stop=True)
                mm.then_inc(s_done, 1)

            def turn(W, s):
                pe.wait_ge(sub_done, W + 1)
                if not (isinstance(W, int) and W < 2):
                    pe.wait_ge(exp_done, W - 1)
                for hp in range(NH // 2):
                    mm = pe.transpose(ps_t[s][0:WK, hp * P:hp * P + WQ],
                                      d[0:WQ, s, 2 * hp:2 * hp + 2, :].rearrange("p a b -> p (a b)")[:, 0:WK],
                                      ident[0:WQ, 0:WQ])
                mm.then_inc(t_done, 1)

            def values(W, R, par, a):
                s = a % 2
                pe.wait_ge(exp_done, W + 1)
                if a == 0:
                    pe.wait_ge(v_ready, R + 1)
                if a % 2 == 0 and not (isinstance(W, int) and W < 4):
                    pe.wait_ge(o_ready, 2 * R + a // 2 - 1)
                for hp in range(NH // 2):
                    n = (a * 4 + hp) * 2
                    c = (a % 2) * 72 + hp * 18
                    for w in range(2):
                        mm = pe.matmul(ps_o[a // 2][64 * w:64 * w + WT, c:c + 18],
                                       pt[0:WK, s, hp, WT * w:WT * w + WT], vsb[0:WK, par, n + w, :],
                                       start=True, stop=True)
                mm.then_inc(pv_done, 1)

            def gather(R):
                pe.wait_ge(o_ready, 2 * R + 2)
                pe.wait_ge(v_ready, R + 3 if not (isinstance(R, int) and R == NG * NW - 1) else R + 2)
                for m in range(NW // 2):
                    mm = pe.transpose(ps_x[:, m * P:m * P + WK],
                                      osb[0:WK, 2 * m:2 * m + 2].rearrange("p a c -> p (a c)"), ident[0:WK, 0:WK])
                mm.then_inc(ot_done, 1)

            def project(R):
                pe.wait_ge(att_ready, R + 1)
                pe.matmul(ps_x[:, 0:RT], ww("wp"), att[:].rearrange("p a i j -> p i a j"),
                          start=True, stop=True).then_inc(proj_done, 1)

            proj_qk(0, 0)
            proj_v(0, 0)
            pe.wait_ge(ld_fix0, 16 * 4)
            pe.wait_ge(init_dve, 2)
            scores(0, 0, 0, 0, 0)
            proj_qk(1, 1)
            scores(1, 0, 0, 0, 1)

            def body(g, first):
                for r in range(NW):
                    R = g * NW + r
                    W = g * NWIN + r * NW
                    par, nxt = r % 2, (r + 1) % 2
                    turn(W, 0)
                    scores(W + 2, R, r, par, 2)
                    if not (first and r == 0):
                        values(W - 1, R - 1, nxt, 3)
                    proj_v(R + 1, nxt)
                    turn(W + 1, 1)
                    scores(W + 3, R, r, par, 3)
                    values(W, R, par, 0)
                    if not (first and r == 0):
                        gather(R - 1)
                    proj_qk(R + 2, par, nth(1, g - 1) if r == 2 and not first else None)
                    turn(W + 2, 0)
                    if first and r == 0:
                        pe.wait_ge(ld_fix, 16 * 4)
                    scores(W + 4, R + 1, (r + 1) % NW, nxt, 0)
                    values(W + 1, R, par, 1)
                    if not (first and r == 0):
                        project(R - 1)
                    turn(W + 3, 1)
                    scores(W + 5, R + 1, (r + 1) % NW, nxt, 1)
                    values(W + 2, R, par, 2)
                    if r == (0 if first else 1) or (first and r == 2):
                        pe.wait_ge(q_ready, R + 3)
                        pe.wait_ge(ks_ready, R + 3)
                    if first and r == 0:
                        mix(1, 1, 2, ps_qk)
                    if first and r == 2:
                        pe.wait_ge(asum_ready, 1)
                        pe.matmul(ps_qk[:, C:2 * C], cc("ones"), asum[:], start=True, stop=True).then_inc(pe_alpha, 1)
                        mix(2, 2, 3, ps_qk)
                    if r == 1 and not first:
                        mix(col(1, 0), 1, nth(1, g - 1), ps_qk)

            body(0, True)
            with pe.Fori(1, NG) as g:
                body(g, False)
            def conv_bank(u):
                if u >= 4:
                    pe.wait_ge(x_done, u - 3)
                return bk[u % 4]

            def conv1(g, i):
                if i == 0:
                    pe.wait_ge(sg_ready, g + 1)
                ps = conv_bank(2 * g + i)
                for tap in range(NTAP):
                    ky, kx = tap // 3, tap % 3
                    mm = pe.matmul(ps[:, 0:HALF], w1[:, tap, :],
                                   sg1[:, g, ky + i * HR:ky + (i + 1) * HR, kx:kx + HW],
                                   start=(tap == 0), stop=(tap == NTAP - 1))
                mm.then_inc(conv_done, 1)

            def conv2_stacked(g, i):
                if i == 0:
                    pe.wait_ge(stacked[g % 2], stacked_by(g))
                    if g == 0:
                        pe.wait_ge(p2_placed, 2)
                ps = conv_bank(2 * NG + 2 * g + i)
                for tap in range(NTAP):
                    ky, kx = tap // 3, tap % 3
                    for w in range(2):
                        pe.matmul(ps[64 * w:64 * w + 64, 0:HALF], w2[:, tap],
                                  p12[:, g % 2, w, ky + i * HR:ky + (i + 1) * HR, kx:kx + HW],
                                  start=(tap == 0), stop=False)

            def conv2_third(g, i):
                if i == 0:
                    pe.wait_ge(p3_ready, g + 1)
                    if g > 0:
                        pe.wait_ge(thirds_stacked[g % 2], 16 * 4 * ((g + 1) // 2))
                ps = bk[(2 * NG + 2 * g + i) % 4]
                if g > 0:
                    for kx in range(3):
                        for w in range(2):
                            pe.matmul(ps[64 * w:64 * w + 64, 0:HALF], w2b[:, kx],
                                      p33[:, g % 2, w, i * HR:(i + 1) * HR, kx:kx + HW], start=False, stop=False)
                for tap in range(0 if g == 0 else 6, NTAP):
                    ky, kx = tap // 3, tap % 3
                    for w in range(2):
                        q = slice(64 * w, 64 * w + 64)
                        mm = pe.matmul(ps[q, 0:HALF], w2[q, tap],
                                       parts[q, g % 2, 2, ky + i * HR:ky + (i + 1) * HR, kx:kx + HW],
                                       start=False, stop=(tap == NTAP - 1))
                mm.then_inc(conv_done, 1)

            def conv2(g):
                for i in range(2):
                    conv2_stacked(g, i)
                for i in range(2):
                    conv2_third(g, i)

            def channel_sums(g, i):
                if i == 0:
                    pe.wait_ge(box_ready, g + 1)
                u = 2 * g + i
                if u >= 2:
                    pe.wait_ge(ka_ready, u - 1)
                pe.matmul(bk[4 + i][:, 0:HALF], aw[:], v2[:, g, i * HR:(i + 1) * HR, :],
                          start=True, stop=True).then_inc(ka_done, 1)

            last = NG * NW - 1
            values(NG * NWIN - 1, last, 1, 3)
            pe.wait_ge(sub_done, NG * NWIN + 1)
            pe.wait_ge(w1_ready, 2)
            channel_sums(0, 0)
            conv1(0, 0)
            gather(last)
            channel_sums(0, 1)
            conv1(0, 1)
            project(last)
            conv1(1, 0)
            conv1(1, 1)
            mix(col(1, NG - 1), 1, nth(1, NG - 1), ps_qk)
            channel_sums(1, 0)
            channel_sums(1, 1)
            mix(col(2, 0), 1, nth(2, 0), ps_qk)
            conv1(2, 0)
            conv1(2, 1)
            channel_sums(2, 0)
            channel_sums(2, 1)
            mix(col(2, 1), 1, nth(2, 1), ps_qk)
            conv1(3, 0)
            conv1(3, 1)
            pe.wait_ge(w2_ready, 4)
            conv2_stacked(0, 0)
            channel_sums(3, 0)
            channel_sums(3, 1)
            mix(col(2, 2), 1, nth(2, 2), ps_qk)
            conv2_third(0, 0)
            conv2_stacked(0, 1)
            conv2_third(0, 1)
            mix(col(2, 3), 1, nth(2, 3), ps_qk)
            conv2(1)
            mix(col(3, 0), 1, nth(3, 0), ps_qk)
            conv2(2)
            mix(col(3, 1), 1, nth(3, 1), ps_qk)
            conv2(3)
            mix(col(3, 2), 1, nth(3, 2), ps_qk)
            pe.wait_ge(g12_ready, 1)
            pe.wait_ge(ld_late, 16)

            def expand(v, w):
                g, u, a = v // 2, 2 * v + w, (v % 2) * HALF
                if v % 2 == 0:
                    pe.wait_ge(xs_ready, 2 * g + w + 1)
                    pe.wait_ge(xs_back_ready, 2 * g + w + 1)
                if u >= 2:
                    pe.wait_ge(su_ready, u - 1)
                else:
                    pe.wait_ge(x_done, 4 * NG - 2)
                t = xs[:, g % 2, w]
                pe.matmul(bk[w][:, 0:HALF], g12[:, w, 0], t[:, SHF + a:SHF + a + HALF], start=True, stop=False)
                pe.matmul(bk[w][:, 0:HALF], g12[:, w, 1], t[:, SHF - 2 + a:SHF - 2 + a + HALF],
                          start=False, stop=True).then_inc(u_done, 1)

            def gate_branch(v):
                g, a = v // 2, (v % 2) * HALF
                pe.wait_ge(xs_ready, 2 * g + 2)
                if v >= 1:
                    pe.wait_ge(sz_ready, 2 * v)
                else:
                    pe.wait_ge(x_done, 4 * NG)
                for w in range(2):
                    h = slice(64 * w, 64 * w + 64)
                    mm = pe.matmul(bk[2 + w][:, 0:HALF], ww("wz")[h, :],
                                   xs[h, g % 2, w, SHF + a:SHF + a + HALF], start=True, stop=True)
                mm.then_inc(z_done, 2)

            def contract(v):
                if v >= 2:
                    pe.wait_ge(res_ready, v - 1)
                for w in range(2):
                    pe.wait_ge(y_ready, 2 * v + w + 1)
                    mm = pe.matmul(bk[4 + v % 2][64 * w:64 * w + 64, 0:HALF], ww("wo"), yy[:, 2 * (v % 2) + w, :],
                                   start=True, stop=True)
                mm.then_inc(out_done, 1)

            for v in range(2 * NG):
                expand(v, 0)
                gate_branch(v)
                if 1 <= v < 2 * NG - 1:
                    contract(v - 1)
                expand(v, 1)
                if v == 1:
                    mix(col(3, 3), 1, nth(3, 3), ps_qk)
            contract(2 * NG - 2)
            contract(2 * NG - 1)

        @block.vector
        def _(dve):
            def half_moments(g, b, i):
                return dve.bn_stats(st[:, b, i, :], xflat[:, g, i * HALF:(i + 1) * HALF])

            def merge(b, j):
                return dve.bn_aggr(mv[:, j, :], st[:, b].rearrange("p a b -> p (a b)"))

            def moments(g, layer):
                half_moments(g, g % 2, 0)
                half_moments(g, g % 2, 1).then_inc(bn_done, 1)
                dve.wait_ge(bn_done, NG * layer + g + 1)
                return merge(g % 2, col(layer, g))

            def variances(j, n, count, ps):
                jj = bass.ds(j, n)
                dve.wait_ge(gn_mixed, count)
                dve.tensor_copy(sg[:, jj, 0:2], ps[:, 0:2 * n].rearrange("p (n t) -> p n t", t=2))
                dve.tensor_copy(sg[:, jj, 2], ps[:, 2 * n:3 * n]).then_inc(gn_copied, 1)
                dve.wait_ge(gn_copied, count)
                dve.tensor_tensor(ve[:, jj], sg[:, jj, 2], sg[:, jj, 2], ALU.mult).then_inc(gn_square, 1)
                dve.wait_ge(gn_square, count)
                dve.scalar_tensor_tensor(out=ve[:, jj], in0=ve[:, jj], scalar=EPS, in1=sg[:, jj, 1],
                                         op0=ALU.add, op1=ALU.add).then_inc(gn_var, 1)

            def shifts(j, n, count):
                jj = bass.ds(j, n)
                dve.wait_ge(gn_rstd, count)
                dve.scalar_tensor_tensor(out=nmr[:, jj], in0=sg[:, jj, 0], scalar=-1.0, in1=rstd[:, jj],
                                         op0=ALU.mult, op1=ALU.mult).then_inc(gn_ready, 1)

            dve.memset(warm[:], 0.0).then_inc(warm_set, 1)
            dve.memset(x[:, NG], 0.0)
            dve.memset(rstd[:, NG:NG + 1], 0.0)
            dve.memset(nmr[:, NG:NG + 1], 0.0)
            for b in range(2):
                dve.memset(ps_o[b][:, 0:144], 1.0)
            dve.memset(vsb[:], 0.0).then_inc(vsb_zeroed, 1)
            dve.wait_ge(vsb_zeroed, 1)
            dve.memset(vsb[0:WT, :, :, 8:9], 1.0)
            dve.memset(vsb[64:WK, :, :, 17:18], 1.0).then_inc(init_dve, 1)
            dve.wait_ge(ld_x0, 16)
            moments(0, 0).then_inc(gn_stats, 1)
            variances(0, 1, 1, bk[2])
            dve.wait_ge(ld_w, 16)
            dve.tensor_scalar(bqs[:], ww("bq"), SCALE, None, ALU.mult).then_inc(bqs_ready, 1)
            shifts(0, 1, 1)
            dve.wait_ge(gn_ready, 1)
            dve.wait_ge(init_pool, 1)

            def normalise(g, R, r):
                if not (isinstance(R, int) and R < 2):
                    dve.wait_ge(v_done, R - 1)
                for a, b, s, c, e, t in pieces(r):
                    whole = (e - c) // WS if c == 0 else 0
                    runs = [(c, whole, WS)] if whole else []
                    runs.append((c + whole * WS, 1, e - c - whole * WS))
                    for c0, n, m in runs:
                        t0 = t + c0 - c
                        last = dve.tensor_scalar(
                            xn[:, r % 2, c0 // WS:c0 // WS + n].rearrange("p n (i j) -> p n i j", i=WS)
                            [:, :, a:b, c0 % WS:c0 % WS + m],
                            x[:, g, s:s + b - a, t0:t0 + n * m].rearrange("p i (n j) -> p n i j", n=n),
                            rstd[:, bass.ds(g, 1)], nmr[:, bass.ds(g, 1)], ALU.mult, ALU.add)
                last.then_inc(xn_ready, 1)

            def shift(W, s):
                dve.wait_ge(s_done, W + 1)
                sc = ps_s[s][0:WQ, 0:NH * WT].rearrange("p (h k) -> p h k", k=WT)
                dve.tensor_reduce(mx[0:WQ, s], sc, AXX, ALU.max).then_inc(max_done, 1)
                dve.wait_ge(max_done, W + 1)
                if not (isinstance(W, int) and W < 2):
                    dve.wait_ge(t_done, W - 1)
                dve.tensor_tensor(d[0:WQ, s, :, 0:WT], sc,
                                  mx[0:WQ, s].rearrange("p (h o) -> p h o", o=1).broadcast_to([WQ, NH, WT]),
                                  ALU.subtract).then_inc(sub_done, 1)

            def weigh(R, b):
                dve.wait_ge(pv_done, NW * R + 2 * b + 2)
                o = ps_o[b][0:WK, 0:144].rearrange("p (n h e) -> p n h e", n=2, e=9)
                rcp = rc[0:WK]
                dve.reciprocal(rcp, o[:, :, :, 8]).then_inc(rc_done, 1)
                dve.wait_ge(rc_done, 2 * R + b + 1)
                if b == 0 and not (isinstance(R, int) and R == 0):
                    dve.wait_ge(ot_done, R)
                last = dve.tensor_tensor(
                    osb[0:WK, 2 * b:2 * b + 2].rearrange("p a (h e) -> p a h e", e=HD), o[:, :, :, 0:HD],
                    rcp.rearrange("p n (h o) -> p n h o", o=1).broadcast_to([WK, 2, NH, HD]), ALU.mult)
                last.then_inc(o_ready, 1)

            def residual(g, R, r):
                dve.wait_ge(proj_done, R + 1)
                y = ps_x[:, 0:RT].rearrange("p (i j) -> p i j", j=HW)
                for a, b, s, c, e, t in pieces(r):
                    xx = x[:, g, s:s + b - a, t:t + e - c]
                    last = dve.scalar_tensor_tensor(out=xx, in0=y[:, a:b, c:e], scalar=bt[:, 0:1], in1=xx,
                                                    op0=ALU.add, op1=ALU.add)
                last.then_inc(res_done, 1)

            normalise(0, 0, 0)
            normalise(0, 1, 1)
            dve.memset(d[:, :, :, WT:64], 0.0).then_inc(init_dve, 1)
            dve.wait_ge(pe_bt, 1)
            dve.tensor_tensor(bt[:], bk[3][:, 0:1], ww("bp"), ALU.add).then_inc(bt_ready, 1)
            dve.wait_ge(ks_ready, 1)
            mask_half(dve, 0, 1)
            dve.wait_ge(bt_ready, 1)
            dve.wait_ge(init_dve, 2)
            shift(0, 0)

            def kernel_sums():
                dve.wait_ge(kabs_ready, 1)
                h1f = h1[:].rearrange("p a b -> p (a b)")[:, 0:NTAP * C]
                dve.tensor_reduce(asum[:], h1f.rearrange("p (t c) -> p c t", c=C), AXX, ALU.add)\
                   .then_inc(asum_ready, 1)

            def channel_scales():
                dve.wait_ge(init_pool, 4)
                dve.wait_ge(pe_alpha, 1)
                for w in range(2):
                    q = slice(64 * w, 64 * w + 64)
                    last = dve.tensor_scalar(aw[q, 64 * w:64 * w + 64], ps_qk[q, C:2 * C],
                                             4.0 / (NTAP * C) / (NTAP * C), None, ALU.mult)
                last.then_inc(aw_ready, 1)

            def tap_weights():
                for n in range(4):
                    last = dve.tensor_tensor(g12[:, n // 2, n % 2], ww("wx"), ww("cw")[:, n * P:(n + 1) * P], ALU.mult)
                last.then_inc(g12_ready, 1)

            def body(g, first):
                for r in range(NW):
                    R = g * NW + r
                    W = g * NWIN + r * NW
                    if r == 1 and not first:
                        dve.wait_ge(res_done, R - 1)
                    shift(W + 1, 1)
                    if r == 2 and not first:
                        variances(col(1, 0), 1, nth(1, g - 1), ps_qk)
                    if first and r == 1:
                        variances(1, 1, 2, ps_qk)
                    if first and r == 3:
                        dve.wait_ge(gn_mixed, 3)
                        variances(2, 2, 3, ps_qk)
                        channel_scales()
                    if first and r == 2:
                        shifts(1, 1, 2)
                        kernel_sums()
                        dve.wait_ge(gn_ready, 2)
                    normalise(g if r < 2 else g + 1, R + 2, (r + 2) % NW)
                    if not (first and r == 0):
                        weigh(R - 1, 1)
                    shift(W + 2, 0)
                    if r == 1 and not first:
                        half_moments(g - 1, 0, 0)
                    if r == 2 and not first:
                        dve.tensor_scalar(sg1[:, bass.ds(g - 1, 1), 1:1 + HW, 1:1 + HW], x[:, bass.ds(g - 1, 1)],
                                          sg[:, col(1, 0), 0:1], 0.5, ALU.is_gt, ALU.subtract).then_inc(sg_ready, 1)
                    if first and r == 0:
                        dve.wait_ge(ld_x1, 16)
                        moments(1, 0).then_inc(gn_stats, 1)
                    shift(W + 3, 1)
                    if first and r == 1:
                        moments(2, 0)
                    if first and r == 2:
                        moments(3, 0).then_inc(gn_stats, 1)
                    if r == 1 and not first:
                        half_moments(g - 1, 0, 1).then_inc(bn_done, 1)
                        dve.wait_ge(bn_done, g + NG)
                    if r == 2 and not first:
                        shifts(col(1, 0), 1, nth(1, g - 1))
                    weigh(R, 0)
                    if r == 1 and not first:
                        merge(0, col(1, 0)).then_inc(gn_stats, 1)
                    shift(W + 4, 0)
                    if not (first and r == 0):
                        residual(g if r else g - 1, R - 1, (r - 1) % NW)
                    if r == 3 and first:
                        shifts(2, 2, 3)

            body(0, True)
            dve.wait_ge(gn_ready, 3)
            with dve.Fori(1, NG) as g:
                body(g, False)
            dve.wait_ge(init_pool, 5)

            def finish1(g, i):
                u = 2 * g + i
                xx = xflat[:, g, i * HALF:(i + 1) * HALF]
                dve.wait_ge(conv_done, u + 1)
                dve.wait_ge(ka_ready, u + 1)
                dve.tensor_tensor(prod[:, i], bk[u % 4][:, 0:HALF], ka[:, i], ALU.mult).then_inc(prod_done, 1)
                dve.wait_ge(prod_done, u + 1)
                dve.scalar_tensor_tensor(out=xx, in0=prod[:, i], scalar=ww("b1"), in1=xx, op0=ALU.add,
                                         op1=ALU.add).then_inc(x_done, 1)

            def layer_moments(g, layer):
                dve.wait_ge(x_done, 2 * NG * (layer - 2) + 2 * g + 2)
                moments(g, layer).then_inc(gn_stats, 1)

            def remainder(g):
                s = g % 2
                dve.wait_ge(p1_ready, g + 1)
                dve.tensor_tensor(rem[:, s], xf[:, s], parts[:, s, 0, 1:1 + HW, 1:1 + HW], ALU.subtract)\
                   .then_inc(rem_ready, 1)

            def finish2(g, i):
                u = 2 * NG + 2 * g + i
                xx = xflat[:, g, i * HALF:(i + 1) * HALF]
                dve.wait_ge(conv_done, u + 1)
                dve.tensor_tensor(xx, bk[u % 4][:, 0:HALF], xx, ALU.add).then_inc(x_done, 1)

            def gate(v):
                for w in range(2):
                    u = 2 * v + w
                    dve.wait_ge(su_ready, u + 1)
                    dve.wait_ge(sz_ready, u + 1)
                    if v >= 2:
                        dve.wait_ge(out_done, v - 1)
                    dve.scalar_tensor_tensor(out=yy[:, 2 * (v % 2) + w, :], in0=su[:, u % 2], scalar=4.0,
                                             in1=sz[:, u % 2], op0=ALU.mult, op1=ALU.mult).then_inc(y_ready, 1)

            def stack_front(g, w):
                j = col(3, g)
                if w == 0:
                    dve.wait_ge(gn_ready, nth(3, g))
                    if g >= 2:
                        dve.wait_ge(z_done, 4 * (g - 1))
                q = slice(64 * w, 64 * w + 64)
                dve.tensor_scalar(xs[q, g % 2, w, SHF:SHF + TOK], xflat[q, g], rstd[q, j:j + 1], nmr[q, j:j + 1],
                                  ALU.mult, ALU.add).then_inc(xs_ready, 1)

            def result(v):
                g, i = v // 2, v % 2
                dve.wait_ge(out_done, v + 1)
                dve.tensor_tensor(res[:, g, i * HALF:(i + 1) * HALF], bk[4 + v % 2][:, 0:HALF],
                                  xflat[:, g, i * HALF:(i + 1) * HALF], ALU.add).then_inc(res_ready, 1)

            g = NG - 1
            weigh(NG * NW - 1, 1)
            dve.wait_ge(ld_late, 16)
            finish1(0, 0)
            finish1(0, 1)
            residual(g, NG * NW - 1, NW - 1)
            dve.wait_ge(res_done, NG * NW)
            moments(g, 1).then_inc(gn_stats, 1)
            layer_moments(0, 2)
            variances(col(1, g), 1, nth(1, g), ps_qk)
            dve.tensor_scalar(sg1[:, g, 1:1 + HW, 1:1 + HW], x[:, g], sg[:, col(1, g), 0:1], 0.5,
                              ALU.is_gt, ALU.subtract).then_inc(sg_ready, 1)
            shifts(col(1, g), 1, nth(1, g))
            variances(col(2, 0), 1, nth(2, 0), ps_qk)
            finish1(1, 0)
            shifts(col(2, 0), 1, nth(2, 0))
            finish1(1, 1)
            layer_moments(1, 2)
            remainder(0)
            variances(col(2, 1), 1, nth(2, 1), ps_qk)
            finish1(2, 0)
            shifts(col(2, 1), 1, nth(2, 1))
            finish1(2, 1)
            third_part(dve, 0)
            layer_moments(2, 2)
            remainder(1)
            variances(col(2, 2), 1, nth(2, 2), ps_qk)
            finish1(3, 0)
            shifts(col(2, 2), 1, nth(2, 2))
            finish1(3, 1)
            layer_moments(3, 2)
            remainder(2)
            tap_weights()
            finish2(0, 0)
            variances(col(2, 3), 1, nth(2, 3), ps_qk)
            shifts(col(2, 3), 1, nth(2, 3))
            finish2(0, 1)
            layer_moments(0, 3)
            remainder(3)
            finish2(1, 0)
            variances(col(3, 0), 1, nth(3, 0), ps_qk)
            finish2(1, 1)
            shifts(col(3, 0), 1, nth(3, 0))
            layer_moments(1, 3)
            stack_front(0, 0)
            stack_front(0, 1)
            finish2(2, 0)
            variances(col(3, 1), 1, nth(3, 1), ps_qk)
            finish2(2, 1)
            shifts(col(3, 1), 1, nth(3, 1))
            layer_moments(2, 3)
            stack_front(1, 0)
            stack_front(1, 1)
            finish2(3, 0)
            variances(col(3, 2), 1, nth(3, 2), ps_qk)
            finish2(3, 1)
            shifts(col(3, 2), 1, nth(3, 2))
            layer_moments(3, 3)
            for v in range(2 * NG):
                gate(v)
                if v in (2, 4):
                    for w in range(2):
                        stack_front(v // 2 + 1, w)
                if v >= 1:
                    result(v - 1)
                if v == 1:
                    variances(col(3, 3), 1, nth(3, 3), ps_qk)
                    shifts(col(3, 3), 1, nth(3, 3))
            result(2 * NG - 1)


def pair(a):
    n = a.shape[1]
    o = np.zeros((P, 2, n), a.dtype)
    o[:C, 0] = a
    o[C:, 1] = a
    return o


def constants():
    c = np.zeros((P, NCI), np.float32)
    i = np.arange(P)
    c[i, CI["ident"][0] + i] = 1
    for o, s in ((0, 0.5), (1, 0.5)):
        c[i, CI["avg"][0] + (i ^ o)] = 0.5
    c[i, CI["diff"][0] + i] = 0.5
    c[i, CI["diff"][0] + (i ^ 1)] = -0.5
    c[:C, CI["ones"][0]:CI["ones"][0] + C] = 1
    c[C:, CI["ones"][0] + C:CI["ones"][0] + P] = 1
    c[i, CI["kmask"][0] + (i % 32) // HD] = 1
    late = (np.arange(WS) >= WS - SH).astype(int)
    row, col = np.repeat(late, WS), np.tile(late, WS)
    regions = [row == 0, row == 1, col == 0, col == 1]
    regions += [(row == a) & (col == b) for a in range(2) for b in range(2)]
    qfix = np.zeros((64, NW, NW, WQ), np.float32)
    q = np.arange(WT)
    for r in range(NW):
        for a in range(NW):
            use = {(0, 0): [], (1, 0): [0, 1], (0, 1): [2, 3], (1, 1): [4, 5, 6, 7]}[(r == NW - 1, a == NW - 1)]
            for w in range(2):
                qfix[q, r, a, WT * w + q] = 1
                for k in use:
                    qfix[WT + k, r, a, WT * w:WT * w + WT] = regions[k]
    return c, qfix, np.array(regions)


def kernel(x, L0_conv_qkv_weight, L0_conv_qkv_bias, L0_conv_proj_weight, L0_conv_proj_bias,
           L0_conv_relative_position_bias, L1_conv_kernel, L1_conv_bias, L2_conv_kernel, L3_conv_W_in,
           L3_conv_conv_w, L3_conv_conv_b, L3_conv_W_out):
    import concourse.bacc as bacc
    from concourse.bass_utils import run_bass_kernel_spmd

    f = np.float32
    x = np.asarray(x)
    wqkv, bqkv = np.asarray(L0_conv_qkv_weight), np.asarray(L0_conv_qkv_bias)
    wp, bp = np.asarray(L0_conv_proj_weight), np.asarray(L0_conv_proj_bias)
    rel = np.asarray(L0_conv_relative_position_bias)
    k1, b1 = np.asarray(L1_conv_kernel), np.asarray(L1_conv_bias)
    k2 = np.asarray(L2_conv_kernel)
    win, cw, cb, wo = (np.asarray(a) for a in (L3_conv_W_in, L3_conv_conv_w, L3_conv_conv_b, L3_conv_W_out))

    cst, qfix, regions = constants()
    kfix = np.zeros((2, 64, 4, NW, WT), f)
    for j in range(2):
        kfix[j, 0:WT] = rel[0, 4 * j:4 * j + 4].transpose(1, 0, 2)[:, :, None, :]
        for k, reg in enumerate(regions):
            kfix[j, WT + k] = np.where(reg, 0, -100)

    w = [np.zeros((P, n), f) for n in WIDTHS]

    def put(name, a):
        t, at, n = WI[name]
        w[t][:, at:at + n] = a.reshape(P, n)

    def by_head_half(a):
        return a.reshape(-1, 2, 2, 32).transpose(0, 2, 1, 3).reshape(-1, P)

    both = lambda v: np.concatenate([v, v])
    put("wq", by_head_half(pair(wqkv[0:C].T)))
    put("wk", by_head_half(pair(wqkv[C:2 * C].T)))
    wv = pair(wqkv[2 * C:].T).reshape(P, 2, 4, 2, HD)
    put("wv", wv.transpose(0, 3, 2, 1, 4))
    put("wp", pair(wp.T))
    put("bq", by_head_half(both(bqkv[0:C])[None]))
    put("bk", by_head_half(both(bqkv[C:2 * C])[None]))
    put("bv", both(bqkv[2 * C:]))
    put("bp", both(bp))
    put("b1", both(b1))
    put("cb", cb)
    put("wx", both(win[0:DI].T))
    put("wz", both(win[DI:].T))
    cwt = cw[:, 0, :].T
    near, far = (np.repeat(cwt[None, t], C, 0) for t in ([3, 1], [2, 0]))
    put("cw", np.concatenate([np.concatenate([near, far], 1), np.concatenate([far, near], 1)]))
    put("wo", wo.T)
    taps = lambda k: np.ascontiguousarray(both(k.reshape(NTAP, C, C).transpose(1, 0, 2)))

    arrays = {
        "x_in": np.ascontiguousarray(x.reshape(NG, 2, TOK, C).transpose(1, 3, 0, 2).reshape(P, NG, TOK)),
        "cst_in": cst, "wts_in": w[0], "late_in": w[1], "ker1_in": taps(k1), "ker2_in": taps(k2), "qfix_in": qfix,
        "kfix_in": kfix.reshape(2, 64, 4, RT),
    }
    nc = bacc.Bacc("TRN2", target_bir_lowering=False, num_devices=1)
    args = [nc.dram_tensor(n, a.shape, mybir.dt.from_np(a.dtype), kind="ExternalInput").ap()
            for n, a in arrays.items()]
    args.append(nc.dram_tensor("out", (P, NG, TOK), F32, kind="ExternalOutput").ap())
    program(nc, *args)
    r = run_bass_kernel_spmd(nc, [arrays], core_ids=[0])
    y = np.asarray(r.results[0]["out"]).reshape(2, C, NG, HW, HW)
    return np.ascontiguousarray(y.transpose(2, 0, 3, 4, 1).reshape(2 * NG, HW, HW, C))
```
